# Optimizing a Trainium2 kernel written in Bass

```python
import numpy as np
import jax
import jax.numpy as jnp

def _softmax(x, axis=-1):
    return jax.nn.softmax(x, axis=axis)

def _gelu(x):
    return jax.nn.gelu(x, approximate=True)

def _silu(x):
    return jax.nn.silu(x)

def _sigmoid(x):
    return jax.nn.sigmoid(x)

def _layernorm(x, axis=-1, eps=1e-05):
    m = jnp.mean(x, axis=axis, keepdims=True)
    v = jnp.var(x, axis=axis, keepdims=True)
    return (x - m) / jnp.sqrt(v + eps)

def _scatter_add(tgt, idx, src, axis=0):
    return tgt.at[idx].add(src)

def _segment_sum(src, seg, n):
    return jax.ops.segment_sum(src, seg, n)
kernel_name = 'mk_adaln_d1_jaxref_r2_c5599c'

def setup_inputs(seed: int=0):
    np.random.seed(seed)
    _w = jnp.asarray

    def _L0_attn_setup():
        import jax, jax.numpy as jnp
        import numpy as np
        DT = 0.01
        OMEGA_MAX = 100.0
        key = jax.random.key(seed)
        ks = jax.random.split(key, 7)
        B, T, D, M = (4, 2048, 512, 64)
        N = 2 * M
        u = jax.random.normal(ks[0], (B, T, D), dtype=jnp.float32)
        W_omega = jax.random.normal(ks[1], (M, D), dtype=jnp.float32) * 0.02
        b_omega = jnp.ones((M,), dtype=jnp.float32)
        W_zeta = jax.random.normal(ks[2], (M, D), dtype=jnp.float32) * 0.02
        b_zeta = jnp.zeros((M,), dtype=jnp.float32)
        W_B = jax.random.normal(ks[3], (N, D), dtype=jnp.float32) * (0.1 / np.sqrt(D))
        b_B = jnp.zeros((N,), dtype=jnp.float32)
        C = jax.random.normal(ks[4], (D, N), dtype=jnp.float32) * 0.01
        D_mat = jax.random.normal(ks[5], (D, D), dtype=jnp.float32) * 0.01
        return dict(u=u, W_omega=W_omega, b_omega=b_omega, W_zeta=W_zeta, b_zeta=b_zeta, W_B=W_B, b_B=b_B, C=C, D_mat=D_mat)
    _L0_attn_in = _L0_attn_setup()

    def _L0_ffn_setup():
        import jax, jax.numpy as jnp
        import numpy as np
        DIM = 512

        def _reference_tuple_inner(x, W_r, W_k, W_v, mu_r, mu_k):
            B, T, C = x.shape
            x_prev = jnp.concatenate([jnp.zeros((B, 1, C), x.dtype), x[:, :-1, :]], axis=1)
            xr = mu_r * x + (1.0 - mu_r) * x_prev
            xk = mu_k * x + (1.0 - mu_k) * x_prev
            r = jax.nn.sigmoid(jnp.einsum('btc,dc->btd', xr, W_r))
            k = jnp.einsum('btc,dc->btd', xk, W_k)
            k_act = jnp.square(jax.nn.relu(k))
            out = r * jnp.einsum('btc,dc->btd', k_act, W_v)
            new_state = x[:, -1, :]
            return (out, new_state)
        key = jax.random.key(seed)
        ks = jax.random.split(key, 6)
        B, T, C = (8, 1024, DIM)
        x = jax.random.normal(ks[0], (B, T, C), dtype=jnp.float32)
        s = 1.0 / np.sqrt(C)
        W_r = jax.random.uniform(ks[1], (C, C), jnp.float32, -s, s)
        W_k = jax.random.uniform(ks[2], (C, C), jnp.float32, -s, s)
        W_v = jax.random.uniform(ks[3], (C, C), jnp.float32, -s, s)
        mu_r = jax.random.uniform(ks[4], (C,), jnp.float32)
        mu_k = jax.random.uniform(ks[5], (C,), jnp.float32)
        return {'x': x, 'W_r': W_r, 'W_k': W_k, 'W_v': W_v, 'mu_r': mu_r, 'mu_k': mu_k}
    _L0_ffn_in = _L0_ffn_setup()
    _L0_c = _w((lambda *s: np.random.randn(*s).astype(np.float32) * 0.05)(4, 512))
    _L0_wmod = _w((lambda *s: np.random.randn(*s).astype(np.float32) * 0.05)(512, 6 * 512) * 512 ** (-0.5))
    _d = {'L0_attn_u': _L0_attn_in['u'], 'L0_attn_W_omega': _L0_attn_in['W_omega'], 'L0_attn_b_omega': _L0_attn_in['b_omega'], 'L0_attn_W_zeta': _L0_attn_in['W_zeta'], 'L0_attn_b_zeta': _L0_attn_in['b_zeta'], 'L0_attn_W_B': _L0_attn_in['W_B'], 'L0_attn_b_B': _L0_attn_in['b_B'], 'L0_attn_C': _L0_attn_in['C'], 'L0_attn_D_mat': _L0_attn_in['D_mat'], 'L0_ffn_W_r': _L0_ffn_in['W_r'], 'L0_ffn_W_k': _L0_ffn_in['W_k'], 'L0_ffn_W_v': _L0_ffn_in['W_v'], 'L0_ffn_mu_r': _L0_ffn_in['mu_r'], 'L0_ffn_mu_k': _L0_ffn_in['mu_k'], 'L0_c': _L0_c, 'L0_wmod': _L0_wmod}
    _x0 = _d['L0_attn_u']
    _d['L0_attn_u'] = jax.random.normal(jax.random.fold_in(jax.random.key(seed), 1), (4, 2048, 512), dtype=_x0.dtype)
    del _x0
    return _d

def reference(L0_attn_u, L0_attn_W_omega, L0_attn_b_omega, L0_attn_W_zeta, L0_attn_b_zeta, L0_attn_W_B, L0_attn_b_B, L0_attn_C, L0_attn_D_mat, L0_ffn_W_r, L0_ffn_W_k, L0_ffn_W_v, L0_ffn_mu_r, L0_ffn_mu_k, L0_c, L0_wmod):

    def _L0_attn_ref(u, W_omega, b_omega, W_zeta, b_zeta, W_B, b_B, C, D_mat):
        import jax, jax.numpy as jnp
        import numpy as np
        DT = 0.01
        OMEGA_MAX = 100.0
        B, T, D = u.shape
        M = W_omega.shape[0]
        omega = jax.nn.softplus(jnp.einsum('btd,md->btm', u, W_omega) + b_omega)
        omega = jnp.clip(omega, 0.0001, OMEGA_MAX)
        zeta = jax.nn.sigmoid(jnp.einsum('btd,md->btm', u, W_zeta) + b_zeta)
        A = omega * omega
        S = 1.0 / (1.0 + DT * DT * A)
        d = 1.0 - zeta
        F = jnp.einsum('btd,nd->btn', u, W_B) + b_B

        def step(x, inp):
            A_t, S_t, d_t, F_t = inp
            z = x[:, :M]
            y = x[:, M:]
            z_new = d_t * (S_t * z - DT * A_t * S_t * y)
            y_new = d_t * (DT * S_t * z + S_t * y)
            x_new = jnp.concatenate([z_new, y_new], axis=-1) + F_t
            return (x_new, x_new)
        x0 = jnp.zeros((B, 2 * M), dtype=u.dtype)
        tm = lambda a: jnp.swapaxes(a, 0, 1)
        _, xs = jax.lax.scan(step, x0, (tm(A), tm(S), tm(d), tm(F)))
        xs = jnp.swapaxes(xs, 0, 1)
        y = jnp.einsum('btn,dn->btd', xs, C) + jnp.einsum('bte,de->btd', u, D_mat)
        return y

    def _L0_ffn_ref(x, W_r, W_k, W_v, mu_r, mu_k):
        import jax, jax.numpy as jnp
        import numpy as np
        DIM = 512

        def _reference_tuple_inner(x, W_r, W_k, W_v, mu_r, mu_k):
            B, T, C = x.shape
            x_prev = jnp.concatenate([jnp.zeros((B, 1, C), x.dtype), x[:, :-1, :]], axis=1)
            xr = mu_r * x + (1.0 - mu_r) * x_prev
            xk = mu_k * x + (1.0 - mu_k) * x_prev
            r = jax.nn.sigmoid(jnp.einsum('btc,dc->btd', xr, W_r))
            k = jnp.einsum('btc,dc->btd', xk, W_k)
            k_act = jnp.square(jax.nn.relu(k))
            out = r * jnp.einsum('btc,dc->btd', k_act, W_v)
            new_state = x[:, -1, :]
            return (out, new_state)
        return _reference_tuple_inner(x, W_r, W_k, W_v, mu_r, mu_k)[0]
    x = L0_attn_u
    mod = (_silu(L0_c) @ L0_wmod).reshape(L0_c.shape[0], 6, 1, -1)
    sa, ca, ga, sb, cb, gb = (mod[:, 0], mod[:, 1], mod[:, 2], mod[:, 3], mod[:, 4], mod[:, 5])
    ga = (2 * (ga >= 0) - 1) * jnp.maximum(jnp.abs(ga), 0.25)
    gb = (2 * (gb >= 0) - 1) * jnp.maximum(jnp.abs(gb), 0.25)
    h = _layernorm(x, axis=-1) * (1 + ca) + sa
    x = x + ga * _L0_attn_ref(h, L0_attn_W_omega, L0_attn_b_omega, L0_attn_W_zeta, L0_attn_b_zeta, L0_attn_W_B, L0_attn_b_B, L0_attn_C, L0_attn_D_mat)
    h = _layernorm(x, axis=-1) * (1 + cb) + sb
    x = x + gb * _L0_ffn_ref(h, L0_ffn_W_r, L0_ffn_W_k, L0_ffn_W_v, L0_ffn_mu_r, L0_ffn_mu_k)
    return x

_drawn_inputs = setup_inputs


def setup_inputs(seed=0):
    import zlib

    import numpy as np

    out = dict(_drawn_inputs(seed))
    spreads = {'L0_attn_b_omega': (1.0, 0.6), 'L0_attn_b_zeta': (0.0, 0.8), 'L0_attn_b_B': (0.0, 0.8)}
    factors = {'L0_attn_W_omega': 8.0,
     'L0_attn_W_zeta': 8.0,
     'L0_attn_W_B': 8.0,
     'L0_attn_C': 8.0,
     'L0_ffn_W_r': 8.0,
     'L0_ffn_W_k': 3.042,
     'L0_ffn_W_v': 2.768,
     'L0_ffn_mu_r': 8.0,
     'L0_ffn_mu_k': 5.032}
    for name, (base, spread) in spreads.items():
        noise = np.random.default_rng([zlib.crc32(name.encode()), seed]).standard_normal(out[name].shape)
        drawn = base * np.exp(spread * noise) if base else spread * noise
        out[name] = jnp.asarray(drawn.astype(out[name].dtype))
    for name, factor in factors.items():
        out[name] = (out[name] * factor).astype(out[name].dtype)
    return out
```

```python
from contextlib import ExitStack

import numpy as np

import concourse.bass as bass
from concourse import mybir

F32 = mybir.dt.float32
F32R = mybir.dt.float32r
ALU = mybir.AluOpType
ACT = mybir.ActivationFunctionType

B, T, D, M = 4, 2048, 512, 64
P = 128
KC = D // P
CHUNK, UNIT, HALF = 512, 256, 256
CPB = T // CHUNK
UPB = T // UNIT
NCHUNK, NUNIT = B * CPB, B * UPB
TPU, TPC = UNIT // P, CHUNK // P
LEVELS = HALF.bit_length() - 1
DT, OMEGA_MIN, OMEGA_MAX, EPS, GATE_MIN = 0.01, 1e-4, 100.0, 1e-5, 0.25
EXP_CAP = 1e30
A_R, A_K, B_R, B_K, SHIFT, FIRST_R, FIRST_K, NTAB = 0, 4, 8, 12, 16, 20, 24, 28
STEP_NEG_ABS, STEP_COEFFS = 3, 11
STEP_TREE = STEP_COEFFS + 11 + 4 * (LEVELS - 1)
STEP_ROOTS = STEP_TREE + 8
STEPS = STEP_ROOTS + 3 * (LEVELS - 1) + 5
EVEN_SOLO, ODD_SOLO = 20, 8
SPLIT_LEVEL = 3
EDGES = 3 + 5 * (UPB - 1)


def build(nc, d):
    ctx = ExitStack()
    with ctx:
        def sb(name, shape, dt=F32):
            return ctx.enter_context(nc.sbuf_tensor(name, shape, dt))

        def sem(name):
            return ctx.enter_context(nc.semaphore(name))

        proj = [sb(f"proj_{n}", [P, KC, 256], F32R) for n in ("hi", "lo")]
        wd = [sb(f"wd_{n}", [P, KC, D], F32R) for n in ("hi", "lo")]
        wc = [sb(f"wc_{n}", [P, D], F32R) for n in ("hi", "lo")]
        wk = [sb(f"wk_{n}", [P, KC, D], F32R) for n in ("hi", "lo")]
        wr = [sb(f"wr_{n}", [P, KC, D], F32R) for n in ("hi", "lo")]
        wv = [sb(f"wv_{n}", [P, KC, D], F32R) for n in ("hi", "lo")]
        ident = sb("ident", [P, P])
        scan_bias = sb("scan_bias", [P, 4])
        mu = sb("mu", [P, 2, KC])
        one_minus_mu = sb("one_minus_mu", [P, 2, KC])
        silu_c = sb("silu_c", [P, KC, B])
        c_in = sb("c_in", [P, KC, B])
        tab_h = sb("tab_h", [P, B, 2 * KC])
        tab_m = sb("tab_m", [P, B, NTAB])
        cb1 = sb("cb1", [P, B, KC])
        cur_h = sb("cur_h", [P, 2 * KC])
        cur_m = sb("cur_m", [P, NTAB])
        gate_a = sb("gate_a", [P, D])
        gate_b = sb("gate_b", [P, D])
        inv_d, eps, minus_half = (sb(n, [P, TPC]) for n in ("inv_d", "eps", "minus_half"))

        x_in = sb("x_in", [P, TPC, D])
        sum1 = sb("sum1", [P, TPC])
        neg_mean1 = sb("neg_mean1", [P, TPC])
        sq1 = sb("sq1", [P, TPC])
        var1 = sb("var1", [P, TPC])
        square_out = sb("square_out", [P, 2, D], mybir.dt.bfloat16)
        rstd1 = sb("rstd1", [P, TPC])
        h_full = sb("h_full", [P, KC, CHUNK])
        h = [[sb(f"h_{n}{i}", [P, KC, CHUNK], F32R) for n in ("hi", "lo")] for i in range(2)]

        x2 = sb("x2", [P, 4, TPU, D])
        stage = x2[:, :, :, :].rearrange("p (s a) t n -> p s (a t) n", s=2)
        sum2 = sb("sum2", [P, TPU])
        neg_mean2 = sb("neg_mean2", [P, TPU])
        sq2 = sb("sq2", [P, TPU])
        var2 = sb("var2", [P, TPU])
        rstd2 = sb("rstd2", [P, TPU])
        xn2 = sb("xn2", [P, TPU, D])
        last_n = sb("last_n", [P, KC])
        mix = [sb(f"mix_{n}", [P, KC, UNIT]) for n in "kr"]
        mixs = [[sb(f"mix_{n}_{m}", [P, KC, UNIT], F32R) for m in ("hi", "lo")] for n in "kr"]
        kk = sb("kk", [P, 2, 2 * UNIT])
        kks = [sb(f"kk_{m}", [P, KC, UNIT], F32R) for m in ("hi", "lo")]
        rt = sb("rt", [P, TPU, D])

        om = sb("om", [P, HALF])
        om_pos = sb("om_pos", [P, HALF])
        om_exp = sb("om_exp", [P, HALF])
        ze = sb("ze", [P, HALF])
        hh = sb("hh", [P, HALF])
        ee = sb("ee", [P, HALF])
        f0 = sb("f0", [P, 2, HALF])
        tree = [None] + [sb(f"tree{l}", [P, 2, 3, HALF >> l]) for l in range(1, LEVELS + 1)]
        tmp0 = sb("tmp0", [P, 384])
        tmp1 = sb("tmp1", [P, 384])
        state = sb("state", [P, 2, HALF + 1])
        xs = sb("xs", [P, CHUNK])
        xss = [sb(f"xs_{m}", [P, CHUNK], F32R) for m in ("hi", "lo")]

        def banks(name):
            return ctx.enter_context(nc.psum_tensor(name, [P, 2, 512], F32))

        ps_kr, ps_tv, ps_pt, ps_cd = banks("ps_kr"), banks("ps_tv"), banks("ps_pt"), banks("ps_cd")

        s_const = sem("s_const")
        s_stage = [sem(f"s_stage{i}") for i in range(2)]
        s_piece = sem("s_piece")
        s_mod_mm = sem("s_mod_mm")
        s_prep = sem("s_prep")
        s_silu = sem("s_silu")
        s_rows = sem("s_rows")
        s_gate_a, s_gate_b = sem("s_gate_a"), sem("s_gate_b")
        s_pool_const = sem("s_pool_const")
        s_cur_h, s_cur_m = sem("s_cur_h"), sem("s_cur_m")
        s_xin = sem("s_xin")
        s_sum1 = sem("s_sum1")
        s_mean1 = sem("s_mean1")
        s_sq1 = sem("s_sq1")
        s_var1 = sem("s_var1")
        s_rstd1 = sem("s_rstd1")
        s_xn1 = sem("s_xn1")
        s_t1 = sem("s_t1")
        s_h = sem("s_h")
        s_h_hi, s_h_lo = sem("s_h_hi"), sem("s_h_lo")
        s_p = sem("s_p")
        s_pev = sem("s_pev")
        s_zexp = sem("s_zexp")
        s_wexp = sem("s_wexp")
        s_softln = sem("s_softln")
        s_rec = sem("s_rec")
        s_xs = sem("s_xs")
        s_xs_hi, s_xs_lo = sem("s_xs_hi"), sem("s_xs_lo")
        s_x2in = [sem(f"s_x2in{r}") for r in range(4)]
        s_cd = sem("s_cd")
        s_gated = sem("s_gated")
        s_x2 = sem("s_x2")
        s_mean2, s_sq2, s_var2 = sem("s_mean2"), sem("s_sq2"), sem("s_var2")
        s_rstd2 = sem("s_rstd2")
        s_xn2 = sem("s_xn2")
        s_t2 = sem("s_t2")
        s_prev = sem("s_prev")
        s_edge = sem("s_edge")
        s_mix = sem("s_mix")
        s_mix_hi = [sem("s_mix_k_hi"), sem("s_mix_r_hi")]
        s_mix_lo = [sem("s_mix_k_lo"), sem("s_mix_r_lo")]
        s_k, s_r, s_v = sem("s_k"), sem("s_r"), sem("s_v")
        s_relu, s_kk = sem("s_relu"), sem("s_kk")
        s_kk_hi, s_kk_lo = sem("s_kk_hi"), sem("s_kk_lo")
        s_rt = sem("s_rt")
        s_rv = sem("s_rv")
        s_rvg = sem("s_rvg")
        s_out = sem("s_out")
        s_stored = sem("s_stored")

        x_rows = d["x"].rearrange("(q i p) n -> q p i n", p=P, i=TPC)
        x_units = d["x"].rearrange("(u i p) n -> u p i n", p=P, i=TPU)
        out_units = d["out"].rearrange("(u i p) n -> u p i n", p=P, i=TPU)
        rows = d["gate_rows"]

        def mod_piece(v):
            return d["wmod"][:, v * D:(v + 1) * D].rearrange("(k p) n -> p k n", p=P)

        def weight_piece(name):
            return d[name].rearrange("(k p) n -> p k n", p=P)

        PIECES = ["sa", "ca", "proj", "ga", "wd", "wc", "sb", "cb", "gb", "wk", "wr", "wv"]
        MOD = {"sa": 0, "ca": 1, "ga": 2, "sb": 3, "cb": 4, "gb": 5}
        MODS = [p for p in PIECES if p in MOD]
        N_STAGED = {0: 0, 1: 0}
        LANDED = {}
        for n, what in enumerate(PIECES):
            N_STAGED[n % 2] += 16 * (3 if what == "proj" else 1)
            LANDED[what] = (n % 2, N_STAGED[n % 2])

        block = ctx.enter_context(nc.Block())

        def piece_done(what):
            return PIECES.index(what) + 1

        @block.sync
        def _(sp):
            sp.dma_start(c_in[:, :, :], d["c"]).then_inc(s_const, 16)
            sp.dma_start(x_in[:, :, :], x_rows[0]).then_inc(s_xin, 16)
            sp.dma_start(ident[:, :], d["ident"]).then_inc(s_const, 16)
            sp.dma_start(scan_bias[:, :], d["scan_bias"]).then_inc(s_const, 16)
            sp.dma_start(mu[:, :, :], d["mu"]).then_inc(s_const, 16)
            for n, what in enumerate(PIECES):
                if n >= 2:
                    sp.wait_ge(s_piece, n - 1)
                st, s = stage[:, n % 2], s_stage[n % 2]
                if what in MOD:
                    sp.dma_start(st, mod_piece(MOD[what])).then_inc(s, 16)
                elif what == "proj":
                    for name, at, w in (("w_omega", 0, M), ("w_zeta", M, M), ("w_b", 2 * M, 2 * M)):
                        sp.dma_start(st[:, :, at:at + w], weight_piece(name)).then_inc(s, 16)
                elif what == "wc":
                    sp.dma_start(st[:, 0, :], d["wc"]).then_inc(s, 16)
                else:
                    sp.dma_start(st, weight_piece(what)).then_inc(s, 16)
                if what in ("wd", "wc"):
                    q = 1 if what == "wd" else 2
                    sp.wait_ge(s_t1, q * KC)
                    sp.dma_start(x_in[:, :, :], x_rows[q]).then_inc(s_xin, 16)
            sp.wait_ge(s_piece, piece_done("gb"))
            sp.dma_start(rows[0], xn2[0:B, 0, :]).then_inc(s_rows, 16)
            sp.dma_start(rows[1], xn2[0:B, 1, :]).then_inc(s_rows, 16)
            sp.wait_ge(s_rows, 32)
            sp.dma_start(gate_a[:, :], rows[0, 0:1, :].partition_broadcast(P)).then_inc(s_gate_a, 16)
            sp.dma_start(gate_b[:, :], rows[1, 0:1, :].partition_broadcast(P)).then_inc(s_gate_b, 16)
            sp.wait_ge(s_piece, len(PIECES))
            for u in range(3):
                sp.dma_start(x2[:, u], x_units[u]).then_inc(s_x2in[u], 16)
            sp.sem_inc(s_stored, 16)

            def slots(b, last):
                for s in range(UPB):
                    u = b * UPB + s
                    if s == 6 and not last:
                        sp.wait_ge(s_gated, (b + 1) * (UPB * TPU))
                        sp.dma_start(gate_a[:, :], rows[0, bass.ds(b + 1, 1), :].partition_broadcast(P))\
                          .then_inc(s_gate_a, 16)
                    if not (last and s + 3 >= UPB):
                        sp.wait_ge(s_stored, u * 16 + 16)
                        sp.dma_start(x2[:, (s + 3) % 4], x_units[u + 3]).then_inc(s_x2in[(s + 3) % 4], 16)
                    if s % 2 == 0 and not (last and s // 2 + 3 >= CPB):
                        q = b * CPB + s // 2 + 3
                        sp.wait_ge(s_t1, q * KC)
                        sp.dma_start(x_in[:, :, :], x_rows[q]).then_inc(s_xin, 16)
                    sp.wait_ge(s_out, u * TPU + 2 * TPU)
                    sp.dma_start(out_units[u], x2[:, s % 4]).then_inc(s_stored, 16)
                if not last:
                    sp.dma_start(gate_b[:, :], rows[1, bass.ds(b + 1, 1), :].partition_broadcast(P))\
                      .then_inc(s_gate_b, 16)

            with sp.Fori(0, B - 1) as b:
                slots(b, False)
            slots(B - 1, True)
            sp.wait_ge(s_stored, 16 * (NUNIT + 1))

        @block.tensor
        def _(pe):
            def product(out, act, weight, acc0=True, acc1=True):
                n = len(act[0])
                mm = None
                for a, w in ((0, 0), (0, 1), (1, 0)):
                    for k in range(n):
                        mm = pe.matmul(out, act[a][k], weight[w][k],
                                       start=acc0 and a == 0 and w == 0 and k == 0,
                                       stop=acc1 and a == 1 and k == n - 1)
                return mm

            def t1_blocks(q, ks):
                for k in ks:
                    for i in range(TPC):
                        mm = pe.transpose(ps_pt[:, k % 2, i * P:(i + 1) * P],
                                          x_in[:, i, k * P:(k + 1) * P], ident[:, :])
                    mm.then_inc(s_t1, 1)

            def projections(q, par):
                pe.wait_ge(s_h_hi, q * KC + KC)
                pe.wait_ge(s_h_lo, q * KC + KC)
                for m in range(2):
                    product(ps_pt[:, m, :],
                            [[proj[w][:, k, m * P:(m + 1) * P] for k in range(KC)] for w in range(2)],
                            [[h[par][w][:, k, :] for k in range(KC)] for w in range(2)]).then_inc(s_p, 1)

            def state_output(b, s):
                par, at = (s // 2) % 2, (s % 2) * UNIT
                for i in range(TPU):
                    t = slice(at + i * P, at + (i + 1) * P)
                    product(ps_cd[:, i, :],
                            [[h[par][w][:, k, t] for k in range(KC)] + [xss[w][:, t]] for w in range(2)],
                            [[wd[w][:, k, :] for k in range(KC)] + [wc[w][:, :]] for w in range(2)])\
                        .then_inc(s_cd, 1)

            def t2_blocks(u):
                pe.wait_ge(s_xn2, u * TPU + TPU)
                for k in range(KC):
                    for i in range(TPU):
                        at = (k % 2) * UNIT + i * P
                        mm = pe.transpose(ps_tv[:, k // 2, at:at + P], xn2[:, i, k * P:(k + 1) * P],
                                          ident[:, :])
                    mm.then_inc(s_t2, 1)

            def modulation(what):
                half, landed = LANDED[what]
                pe.wait_ge(s_stage[half], landed)
                w = stage[:, half]
                if what in ("ga", "gb"):
                    for k in range(KC):
                        mm = pe.matmul(ps_cd[0:B, 0, :], silu_c[:, k, :], w[:, k, :],
                                       start=(k == 0), stop=(k == KC - 1))
                else:
                    for m in range(KC):
                        for k in range(KC):
                            mm = pe.matmul(ps_cd[:, 0, m * B:(m + 1) * B], w[:, k, m * P:(m + 1) * P],
                                           silu_c[:, k, :], start=(k == 0), stop=(k == KC - 1))
                mm.then_inc(s_mod_mm, 1)

            def transposed_in(q):
                pe.wait_ge(s_xn1, TPC * (q + 1))
                t1_blocks(q, (0, 1))
                for k in (2, 3):
                    pe.wait_ge(s_h, q * KC + k - 1)
                    t1_blocks(q, (k,))

            pe.wait_ge(s_const, 64)
            pe.wait_ge(s_silu, 2)
            modulation("sa")
            pe.wait_ge(s_piece, piece_done("sa"))
            modulation("ca")
            transposed_in(0)
            for q in range(2):
                pe.wait_ge(s_h, (q + 1) * KC)
                pe.wait_ge(s_piece, piece_done("proj"))
                projections(q, q)
                pe.wait_ge(s_pev, q + 1)
                transposed_in(q + 1)
                if q == 0:
                    pe.wait_ge(s_piece, piece_done("ca"))
                    modulation("ga")
            for what, before in (("sb", "ga"), ("cb", "sb"), ("gb", "cb")):
                pe.wait_ge(s_piece, piece_done(before))
                modulation(what)
            pe.wait_ge(s_xs_hi, 1)
            pe.wait_ge(s_xs_lo, 1)
            pe.wait_ge(s_piece, piece_done("gb"))
            state_output(0, 0)
            t2_blocks(0)
            pe.wait_ge(s_gated, TPU)
            state_output(1, 1)

            def k_product(u):
                pe.wait_ge(s_mix_hi[0], u * 2 + 2)
                pe.wait_ge(s_mix_lo[0], u * 2 + 2)
                pe.wait_ge(s_rt, u * TPU + TPU)
                for m in range(KC):
                    mm = product(ps_kr[:, m // 2, (m % 2) * UNIT:(m % 2 + 1) * UNIT],
                                 [[wk[w][:, k, m * P:(m + 1) * P] for k in range(KC)] for w in range(2)],
                                 [[mixs[0][w][:, k, :] for k in range(KC)] for w in range(2)])
                    if m % 2:
                        mm.then_inc(s_k, 1)

            def r_product(u):
                pe.wait_ge(s_mix_hi[1], u * 2 + 2)
                pe.wait_ge(s_mix_lo[1], u * 2 + 2)
                pe.wait_ge(s_relu, u * 2 + 2)
                for i in range(TPU):
                    product(ps_kr[:, i, :],
                            [[mixs[1][w][:, k, i * P:(i + 1) * P] for k in range(KC)] for w in range(2)],
                            [[wr[w][:, k, :] for k in range(KC)] for w in range(2)]).then_inc(s_r, 1)

            def v_product(u, mixes_before):
                pe.wait_ge(s_kk_hi, u * 2 + 2)
                pe.wait_ge(s_kk_lo, u * 2 + 2)
                if mixes_before:
                    pe.wait_ge(s_mix, u * 2 * KC + 4 * KC)
                else:
                    pe.wait_ge(s_rv, u * TPU + TPU)
                for i in range(TPU):
                    product(ps_tv[:, i, :],
                            [[kks[w][:, k, i * P:(i + 1) * P] for k in range(KC)] for w in range(2)],
                            [[wv[w][:, k, :] for k in range(KC)] for w in range(2)]).then_inc(s_v, 1)

            def slots(b, last):
                for s in range(UPB):
                    u, q = b * UPB + s, b * CPB + s // 2
                    t1 = s % 2 == 1 and not (last and s // 2 + 3 >= CPB)
                    if s == 0:
                        pe.wait_ge(s_piece, len(PIECES))
                    k_product(u)
                    if t1:
                        pe.wait_ge(s_xn1, q * TPC + 4 * TPC)
                        pe.wait_ge(s_pev, q + 3)
                        t1_blocks(q + 3, (0, 1))
                    if not (last and s + 1 >= UPB):
                        pe.wait_ge(s_rv, u * TPU + TPU)
                        t2_blocks(u + 1)
                    if s % 2 == 0:
                        if not (last and s // 2 + 2 >= CPB):
                            pe.wait_ge(s_h, q * KC + 3 * KC)
                            projections(q + 2, (s // 2) % 2)
                        r_product(u)
                    if not (last and s + 2 >= UPB):
                        if s % 2 == 0:
                            pe.wait_ge(s_xs_hi, q + 2)
                            pe.wait_ge(s_xs_lo, q + 2)
                        pe.wait_ge(s_gated, u * TPU + 2 * TPU)
                        state_output(u + 2, (s + 2) % UPB)
                    if t1:
                        for k in (2, 3):
                            pe.wait_ge(s_h, q * KC + 3 * KC + k - 1)
                            t1_blocks(q + 3, (k,))
                    if s % 2 == 1:
                        r_product(u)
                    v_product(u, not (last and s + 1 >= UPB))

            with pe.Fori(0, B - 1) as b:
                slots(b, False)
            slots(B - 1, True)

        @block.scalar
        def _(act):
            def h_blocks(q, ks):
                for k in ks:
                    act.wait_ge(s_t1, q * KC + k + 1)
                    act.activation(h_full[:, k, :], ps_pt[:, k % 2, :], ACT.Identity,
                                   bias=cur_h[:, KC + k:KC + k + 1], scale=cur_h[:, k:k + 1]).then_inc(s_h, 1)

            def squares(x, neg_mean, out, count, s_sq):
                for i in range(out.shape[1]):
                    if i >= 2:
                        act.wait_ge(s_sq, count + i - 1)
                    act.activation(square_out[:, i % 2, :], x[:, i, :], ACT.Square, bias=neg_mean[:, i:i + 1],
                                   accum_out=out[:, i:i + 1]).then_inc(s_sq, 1)

            def statistics1(q):
                act.wait_ge(s_xin, q * 16 + 16)
                for i in range(TPC):
                    act.activation(x_in[:, i, :], x_in[:, i, :], ACT.Identity, accum_out=sum1[:, i:i + 1])\
                       .then_inc(s_sum1, 1)
                act.wait_ge(s_sum1, q * TPC + TPC)
                act.activation(neg_mean1[:, :], sum1[:, :], ACT.Identity, scale=-1.0 / D).then_inc(s_mean1, 1)
                act.wait_ge(s_mean1, q + 1)
                squares(x_in, neg_mean1, sq1, q * TPC, s_sq1)

            def statistics2(b, s):
                u = b * UPB + s
                act.wait_ge(s_x2, u * TPU + TPU)
                act.activation(neg_mean2[:, :], sum2[:, :], ACT.Identity, scale=-1.0 / D).then_inc(s_mean2, 1)
                act.wait_ge(s_mean2, u + 1)
                squares(x2[:, s % 4], neg_mean2, sq2, u * TPU, s_sq2)

            def projections_out(q):
                act.wait_ge(s_p, q * 2 + 2)
                for half in range(2):
                    to, cols = slice(half * M, half * M + M), slice(half * HALF, (half + 1) * HALF)
                    act.activation(om[to, :], ps_pt[0:M, 0, cols], ACT.Identity)
                    act.activation(ze[to, :], ps_pt[M:2 * M, 0, cols], ACT.Identity)
                    act.activation(f0[to, 0, :], ps_pt[0:M, 1, cols], ACT.Identity)
                    mm = act.activation(f0[to, 1, :], ps_pt[M:2 * M, 1, cols], ACT.Identity)
                mm.then_inc(s_pev, 1)

            def softplus_parts(q):
                act.wait_ge(s_pev, q + 1)
                act.activation(ze[:, :], ze[:, :], ACT.Exp, bias=scan_bias[:, 1:2]).then_inc(s_zexp, 1)
                act.wait_ge(s_rec, q * STEPS + STEP_NEG_ABS)
                act.activation(om_exp[:, :], om_exp[:, :], ACT.Exp).then_inc(s_wexp, 1)
                act.wait_ge(s_wexp, q + 1)
                act.activation(om_exp[:, :], om_exp[:, :], ACT.Ln, bias=1.0).then_inc(s_softln, 1)

            def states_out(q, first):
                act.wait_ge(s_rec, q * STEPS + STEPS)
                if not first:
                    act.wait_ge(s_xs_hi, q)
                    act.wait_ge(s_xs_lo, q)
                for half in range(2):
                    frm, cols = slice(half * M, half * M + M), slice(half * HALF, (half + 1) * HALF)
                    act.activation(xs[0:M, cols], state[frm, 0, 1:HALF + 1], ACT.Identity)
                    mm = act.activation(xs[M:2 * M, cols], state[frm, 1, 1:HALF + 1], ACT.Identity, scale=DT)
                mm.then_inc(s_xs, 1)

            def shifted(u, first):
                if not first:
                    for n in range(2):
                        act.wait_ge(s_mix_hi[n], u * 2)
                        act.wait_ge(s_mix_lo[n], u * 2)
                for j in range(2):
                    act.wait_ge(s_t2, u * KC + 2 * j + 2)
                    for n, beta in ((0, B_K), (1, B_R)):
                        for c in range(2):
                            k = 2 * j + c
                            mm = act.activation(mix[n][:, k, 1:UNIT], ps_tv[:, j, c * UNIT:(c + 1) * UNIT - 1],
                                                ACT.Identity, bias=cur_m[:, SHIFT + k:SHIFT + k + 1],
                                                scale=cur_m[:, beta + k:beta + k + 1])
                    mm.then_inc(s_prev, 1)

            act.sem_inc(s_rt, TPU)
            act.wait_ge(s_const, 64)
            act.activation(silu_c[:, :, :], c_in[:, :, :], ACT.Exp, scale=-1.0).then_inc(s_silu, 1)
            statistics1(0)
            act.wait_ge(s_cur_h, 1)
            h_blocks(0, range(KC))
            statistics1(1)
            for q in range(2):
                projections_out(q)
                act.wait_ge(s_h_hi, (q + 1) * KC)
                act.wait_ge(s_h_lo, (q + 1) * KC)
                h_blocks(q + 1, range(KC))
                softplus_parts(q)
                if q == 0:
                    statistics1(2)
                    states_out(0, True)
            statistics2(0, 0)
            act.wait_ge(s_cur_m, 1)
            shifted(0, True)
            statistics2(0, 1)

            def slots(b, last):
                for s in range(UPB):
                    u = b * UPB + s
                    q = b * CPB + s // 2
                    act.wait_ge(s_rv, u * TPU + TPU)
                    for i in range(2):
                        act.wait_ge(s_k, u * 2 + i + 1)
                        act.activation(kk[:, i, :], ps_kr[:, i, :], ACT.Relu).then_inc(s_relu, 1)
                    for i in range(2):
                        act.wait_ge(s_relu, u * 2 + i + 1)
                        act.activation(kk[:, i, :], kk[:, i, :], ACT.Square).then_inc(s_kk, 1)
                    t1 = s % 2 == 1 and not (last and s // 2 + 3 >= CPB)
                    if t1:
                        if s // 2 + 3 == CPB:
                            act.wait_ge(s_cur_h, b + 2)
                        act.wait_ge(s_h_hi, q * KC + 3 * KC)
                        act.wait_ge(s_h_lo, q * KC + 3 * KC)
                        h_blocks(q + 3, (0, 1))
                    if not (last and s + 1 >= UPB):
                        if s + 1 == UPB:
                            act.wait_ge(s_cur_m, b + 2)
                        shifted(u + 1, False)
                    if s % 2 == 0 and not (last and s + 2 >= UPB):
                        states_out(q + 1, False)
                    p = s % 2 == 0 and not (last and s // 2 + 2 >= CPB)
                    if p:
                        projections_out(q + 2)
                    if t1:
                        h_blocks(q + 3, (2, 3))
                    if s % 2 == 1 and not (last and s + 2 >= UPB):
                        statistics2(b + (s + 2) // UPB, (s + 2) % UPB)
                    act.wait_ge(s_out, u * TPU + TPU)
                    for i in range(TPU):
                        act.wait_ge(s_r, u * TPU + i + 1)
                        act.activation(rt[:, i, :], ps_kr[:, i, :], ACT.Tanh, scale=0.5).then_inc(s_rt, 1)
                    if p:
                        softplus_parts(q + 2)
                    if s % 2 == 0 and not (last and s // 2 + 3 >= CPB):
                        statistics1(q + 3)
                    if s % 2 == 0 and not (last and s + 2 >= UPB):
                        statistics2(b + (s + 2) // UPB, (s + 2) % UPB)

            with act.Fori(0, B - 1) as b:
                slots(b, False)
            slots(B - 1, True)

        @block.vector
        def _(dve):
            def normalise(q):
                dve.wait_ge(s_rstd1, q + 1)
                for i in range(TPC):
                    dve.tensor_scalar(x_in[:, i, :], x_in[:, i, :], neg_mean1[:, i:i + 1], rstd1[:, i:i + 1],
                                      ALU.add, ALU.mult).then_inc(s_xn1, 1)
                    yield

            def h_high(q, par):
                if not (isinstance(q, int) and q < 2):
                    dve.wait_ge(s_cd, q * TPC - TPC)
                for k in range(KC):
                    dve.wait_ge(s_h, q * KC + k + 1)
                    dve.tensor_copy(h[par][0][:, k, :], h_full[:, k, :]).then_inc(s_h_hi, 1)
                    yield

            def states_high(q):
                dve.wait_ge(s_xs, q + 1)
                dve.tensor_copy(xss[0][:, :], xs[:, :]).then_inc(s_xs_hi, 1)

            def new_columns(b, table, cur, s_cur):
                dve.tensor_copy(cur[:, :], table[:, b, :] if isinstance(b, int)
                                else table[:, bass.ds(b, 1), :].rearrange("p a n -> p (a n)")).then_inc(s_cur, 1)

            def mixes(b, s, first):
                u = b * UPB + s
                at = b * EDGES + (0 if s == 0 else 3 + 5 * (s - 1))
                if s == 0:
                    dve.wait_ge(s_cur_m, b + 1)
                if not first:
                    for n in range(2):
                        dve.wait_ge(s_mix_lo[n], u * 2)
                cols = [mix[n][:, :, 0] for n in range(2)]
                if s == 0:
                    dve.tensor_copy(cols[0], cur_m[:, FIRST_K:FIRST_K + KC]).then_inc(s_edge, 1)
                    dve.tensor_copy(cols[1], cur_m[:, FIRST_R:FIRST_R + KC]).then_inc(s_edge, 1)
                    n_edges = 3
                else:
                    dve.tensor_tensor(cols[0], last_n[:, :], cur_m[:, B_K:B_K + KC], ALU.mult).then_inc(s_edge, 1)
                    dve.tensor_tensor(cols[1], last_n[:, :], cur_m[:, B_R:B_R + KC], ALU.mult).then_inc(s_edge, 1)
                    yield
                    for n in range(2):
                        dve.wait_ge(s_edge, at + n + 1)
                        dve.tensor_tensor(cols[n], cols[n], cur_m[:, SHIFT:SHIFT + KC], ALU.add).then_inc(s_edge, 1)
                    n_edges = 5
                yield
                dve.wait_ge(s_edge, at + n_edges - 1)
                for j in range(2):
                    dve.wait_ge(s_prev, u * 2 + j + 1)
                    if j == 1:
                        dve.tensor_copy(last_n[:, :],
                                        ps_tv[:, :, :].rearrange("p a (c t) -> p (a c) t", c=2)[:, :, UNIT - 1])\
                           .then_inc(s_edge, 1)
                        yield
                    for n, alpha in ((0, A_K), (1, A_R)):
                        for c in range(2):
                            k = 2 * j + c
                            dve.scalar_tensor_tensor(mix[n][:, k, :], ps_tv[:, j, c * UNIT:(c + 1) * UNIT],
                                                     cur_m[:, alpha + k:alpha + k + 1], mix[n][:, k, :],
                                                     ALU.mult, ALU.add).then_inc(s_mix, 1)
                            yield
                    yield from mix_high(u, 0, j, first)

            def mix_high(u, n, j, first):
                if j == 0 and not first:
                    dve.wait_ge((s_k, s_r)[n], u * 2)
                dve.wait_ge(s_mix, u * 2 * KC + KC * j + 2 * n + 2)
                dve.tensor_copy(mixs[n][0][:, 2 * j:2 * j + 2, :], mix[n][:, 2 * j:2 * j + 2, :])\
                   .then_inc(s_mix_hi[n], 1)
                yield

            def mix_r_high(u, first):
                for j in range(2):
                    yield from mix_high(u, 1, j, first)

            def residual(b, s, first):
                u = b * UPB + s
                r = s % 4
                if s == 0:
                    dve.wait_ge(s_gate_a, b * 16 + 16)
                if not first:
                    dve.wait_ge(s_t2, u * KC)
                for i in range(TPU):
                    dve.wait_ge(s_cd, u * TPU + i + 1)
                    dve.tensor_tensor(xn2[:, i, :], ps_cd[:, i, :], gate_a[:, :], ALU.mult).then_inc(s_gated, 1)
                    yield
                dve.wait_ge(s_x2in[r], b * (UPB // 4 * 16) + s // 4 * 16 + 16)
                for i in range(TPU):
                    dve.wait_ge(s_gated, u * TPU + i + 1)
                    dve.scalar_tensor_tensor(x2[:, r, i, :], xn2[:, i, :], 1.0, x2[:, r, i, :], ALU.mult, ALU.add,
                                             accum_out=sum2[:, i:i + 1]).then_inc(s_x2, 1)
                    yield

            def normalise2(b, s):
                u = b * UPB + s
                dve.wait_ge(s_rstd2, u + 1)
                for i in range(TPU):
                    dve.tensor_scalar(xn2[:, i, :], x2[:, s % 4, i, :], neg_mean2[:, i:i + 1], rstd2[:, i:i + 1],
                                      ALU.add, ALU.mult).then_inc(s_xn2, 1)
                    yield

            def k_high(u):
                for i in range(2):
                    dve.wait_ge(s_kk, u * 2 + i + 1)
                    dve.tensor_copy(kks[0][:, 2 * i:2 * i + 2, :],
                                    kk[:, i, :].rearrange("p (c t) -> p c t", c=2)).then_inc(s_kk_hi, 1)
                    yield

            def output(b, s):
                u = b * UPB + s
                if s == 0:
                    dve.wait_ge(s_gate_b, b * 16 + 16)
                for i in range(TPU):
                    dve.wait_ge(s_v, u * TPU + i + 1)
                    dve.wait_ge(s_rt, u * TPU + TPU + i + 1)
                    dve.scalar_tensor_tensor(rt[:, i, :], rt[:, i, :], 1.0, ps_tv[:, i, :], ALU.add, ALU.mult)\
                       .then_inc(s_rv, 1)
                    yield
                for i in range(TPU):
                    dve.wait_ge(s_rv, u * TPU + TPU + i + 1)
                    dve.tensor_tensor(rt[:, i, :], rt[:, i, :], gate_b[:, :], ALU.mult).then_inc(s_rvg, 1)
                    yield

            def tmp(t, *shape):
                n = int(np.prod(shape))
                if len(shape) == 3:
                    return t[:, 0:n].rearrange("p (a b c) -> p a b c", a=shape[0], b=shape[1])
                return t[:, 0:n].rearrange("p (a b) -> p a b", a=shape[0])

            def push_down(q, n, after, low, high):
                for l in range(high - 1, low - 1, -1):
                    c = HALF >> (l + 1)
                    step = 2 << l
                    frm = state[:, :, 0:HALF:step]
                    to = state[:, :, 1 << l:HALF:step]
                    if l == 0:
                        e1, h1 = ee[:, 0:HALF:2], hh[:, 0:HALF:2]
                        after(n)
                        dve.tensor_tensor(tmp0[:, 0:c], h1, frm[:, 1, :], ALU.mult).then_inc(s_rec, 1)
                        yield
                        r = tmp(tmp1, 2, c)
                        dve.tensor_tensor(r[:, 1, :], frm[:, 0, :], frm[:, 1, :], ALU.add).then_inc(s_rec, 1)
                        yield
                        after(n + 1)
                        dve.tensor_tensor(r[:, 0, :], frm[:, 0, :], tmp0[:, 0:c], ALU.subtract).then_inc(s_rec, 1)
                        yield
                        after(n + 3)
                        dve.tensor_tensor(r, r, e1.unsqueeze(1).broadcast_to([P, 2, c]), ALU.mult).then_inc(s_rec, 1)
                        yield
                        after(n + 4)
                        dve.tensor_tensor(to, r, f0[:, :, 0:HALF:2], ALU.add).then_inc(s_rec, 1)
                        yield
                        n += 5
                        continue
                    node = tree[l][:, :, :, 0:HALF >> l:2]
                    t, r = tmp(tmp0, 2, 2, c), tmp(tmp1, 2, c)
                    after(n)
                    dve.tensor_tensor(t, node[:, :, 0:2, :], frm.unsqueeze(1).broadcast_to([P, 2, 2, c]),
                                      ALU.mult).then_inc(s_rec, 1)
                    yield
                    after(n + 1)
                    dve.tensor_tensor(r, t[:, :, 0, :], t[:, :, 1, :], ALU.add).then_inc(s_rec, 1)
                    yield
                    after(n + 2)
                    dve.tensor_tensor(to, r, node[:, :, 2, :], ALU.add).then_inc(s_rec, 1)
                    yield
                    n += 3

            def recurrence_up(q, s, first_of_all):
                base = q * STEPS

                def after(n):
                    dve.wait_ge(s_rec, base + n)

                dve.wait_ge(s_pev, q + 1)
                if not first_of_all:
                    dve.wait_ge(s_xs, q)
                bias = [scan_bias[:, i:i + 1] for i in range(4)]
                dve.tensor_scalar(om_pos[:, :], om[:, :], bias[0], 0.0, ALU.add, ALU.max).then_inc(s_rec, 1)
                yield
                dve.tensor_scalar(om[:, :], om[:, :], bias[0], None, ALU.add).then_inc(s_rec, 1)
                yield
                after(2)
                dve.scalar_tensor_tensor(om_exp[:, :], om_pos[:, :], -2.0, om[:, :], ALU.mult, ALU.add)\
                   .then_inc(s_rec, 1)
                yield
                dve.tensor_scalar(f0[:, 0, :], f0[:, 0, :], bias[2], None, ALU.add).then_inc(s_rec, 1)
                yield
                dve.tensor_scalar(f0[:, 1, :], f0[:, 1, :], bias[3], 1.0 / DT, ALU.add, ALU.mult).then_inc(s_rec, 1)
                yield
                dve.wait_ge(s_zexp, q + 1)
                dve.tensor_scalar(ze[:, :], ze[:, :], EXP_CAP, 1.0, ALU.min, ALU.add).then_inc(s_rec, 1)
                yield
                yield
                dve.wait_ge(s_softln, q + 1)
                dve.tensor_tensor(om_pos[:, :], om_pos[:, :], om_exp[:, :], ALU.add).then_inc(s_rec, 1)
                yield
                after(7)
                dve.tensor_scalar(om_pos[:, :], om_pos[:, :], OMEGA_MIN, OMEGA_MAX, ALU.max, ALU.min)\
                   .then_inc(s_rec, 1)
                yield
                after(8)
                dve.scalar_tensor_tensor(hh[:, :], om_pos[:, :], DT * DT, om_pos[:, :], ALU.mult, ALU.mult)\
                   .then_inc(s_rec, 1)
                yield
                after(9)
                dve.scalar_tensor_tensor(ze[:, :], hh[:, :], 1.0, ze[:, :], ALU.add, ALU.mult).then_inc(s_rec, 1)
                yield
                after(10)
                dve.reciprocal(ee[:, :], ze[:, :]).then_inc(s_rec, 1)
                yield
                n, c = STEP_COEFFS, HALF // 2
                e1, e2, h1, h2 = (a[:, i:HALF:2] for a in (ee, hh) for i in range(2))
                f1, f2 = f0[:, :, 0:HALF:2], f0[:, :, 1:HALF:2]
                m = tree[1]
                neg_e, hf, r = tmp0[:, 0:c], tmp0[:, c:2 * c], tmp(tmp1, 2, c)
                dve.tensor_tensor(m[:, 0, 1, :], h1, h2, ALU.add).then_inc(s_rec, 1)
                yield
                dve.tensor_tensor(hf, h2, f1[:, 1, :], ALU.mult).then_inc(s_rec, 1)
                yield
                dve.tensor_tensor(r[:, 1, :], f1[:, 0, :], f1[:, 1, :], ALU.add).then_inc(s_rec, 1)
                yield
                after(n)
                dve.scalar_tensor_tensor(neg_e, e1, -1.0, e2, ALU.mult, ALU.mult).then_inc(s_rec, 1)
                yield
                after(n + 2)
                dve.tensor_tensor(r[:, 0, :], f1[:, 0, :], hf, ALU.subtract).then_inc(s_rec, 1)
                yield
                after(n + 4)
                dve.scalar_tensor_tensor(m[:, 0, 0, :], h2, -1.0, neg_e, ALU.add, ALU.mult).then_inc(s_rec, 1)
                yield
                dve.scalar_tensor_tensor(m[:, 1, 1, :], h1, -1.0, neg_e, ALU.add, ALU.mult).then_inc(s_rec, 1)
                yield
                dve.tensor_scalar(m[:, 1, 0, :], neg_e, -2.0, None, ALU.mult).then_inc(s_rec, 1)
                yield
                dve.tensor_tensor(m[:, 0, 1, :], m[:, 0, 1, :], neg_e, ALU.mult).then_inc(s_rec, 1)
                yield
                after(n + 5)
                dve.tensor_tensor(r, r, e2.unsqueeze(1).broadcast_to([P, 2, c]), ALU.mult).then_inc(s_rec, 1)
                yield
                after(n + 10)
                dve.tensor_tensor(m[:, :, 2, :], r, f2, ALU.add).then_inc(s_rec, 1)
                yield
                n += 11
                for l in range(1, LEVELS):
                    c = HALF >> (l + 1)
                    first, second = tree[l][:, :, :, 0:2 * c:2], tree[l][:, :, :, 1:2 * c:2]
                    t0, t1 = tmp(tmp0, 2, 3, c), tmp(tmp1, 2, 3, c)
                    after(n)
                    for j, t in ((0, t0), (1, t1)):
                        dve.tensor_tensor(t, second[:, :, j:j + 1, :].broadcast_to([P, 2, 3, c]),
                                          first[:, j:j + 1, :, :].broadcast_to([P, 2, 3, c]), ALU.mult)\
                           .then_inc(s_rec, 1)
                        yield
                    after(n + 2)
                    dve.tensor_tensor(tree[l + 1][:, :, :, :], t0, t1, ALU.add).then_inc(s_rec, 1)
                    yield
                    after(n + 3)
                    dve.tensor_tensor(tree[l + 1][:, :, 2, :], tree[l + 1][:, :, 2, :], second[:, :, 2, :],
                                      ALU.add).then_inc(s_rec, 1)
                    yield
                    n += 4
                root = tree[LEVELS][:, :, :, 0]
                t, r = tmp(tmp0, 2, 2), tmp1[:, 0:2]
                lo, up = slice(0, M), slice(M, 2 * M)
                after(n)
                for half, own in ((0, lo), (1, up)):
                    if half == 0 and s == 0:
                        dve.memset(state[lo, :, 0], 0.0).then_inc(s_rec, 1)
                    else:
                        other = (up, lo)[half]
                        dve.tensor_copy(state[own, :, 0], state[other, :, HALF]).then_inc(s_rec, 1)
                    n += 1
                    yield
                    after(n)
                    dve.tensor_tensor(t[own], root[own, :, 0:2], state[own, :, 0].unsqueeze(1).broadcast_to([M, 2, 2]),
                                      ALU.mult).then_inc(s_rec, 1)
                    n += 1
                    yield
                    after(n)
                    dve.tensor_tensor(r[own], t[own, :, 0], t[own, :, 1], ALU.add).then_inc(s_rec, 1)
                    n += 1
                    yield
                    after(n)
                    dve.tensor_tensor(state[own, :, HALF], r[own], root[own, :, 2], ALU.add).then_inc(s_rec, 1)
                    n += 1
                    yield
                    after(n)
                assert n == STEP_ROOTS
                yield from push_down(q, n, after, SPLIT_LEVEL, LEVELS)

            def recurrence_down(q):
                def after(n):
                    dve.wait_ge(s_rec, q * STEPS + n)

                yield from push_down(q, STEP_ROOTS + 3 * (LEVELS - SPLIT_LEVEL), after, 0, SPLIT_LEVEL)

            def run(*steps):
                for g in steps:
                    for _ in g:
                        pass

            def take(steps, count):
                for _ in range(count):
                    next(steps, None)

            def beside(steps, main, per):
                for _ in main:
                    take(steps, per)

            prep = [0]

            def then(ins):
                prep[0] += 1
                ins.then_inc(s_prep, 1)
                dve.wait_ge(s_prep, prep[0])

            def columns(what, out):
                dve.wait_ge(s_mod_mm, MODS.index(what) + 1)
                src = ps_cd[:, 0, 0:KC * B].rearrange("p (k b) -> p b k", k=KC)
                dve.tensor_scalar(out, src, 1.0 if what in ("ca", "cb") else 0.0, None, ALU.add)\
                   .then_inc(s_piece, 1)
                dve.wait_ge(s_piece, piece_done(what))

            def gate(what, row, factor):
                g, sign, size = xn2[0:B, row, :], kk[0:B, 0, :], kk[0:B, 1, :]
                dve.wait_ge(s_mod_mm, MODS.index(what) + 1)
                then(dve.tensor_copy(g, ps_cd[0:B, 0, :]))
                then(dve.tensor_scalar(sign, g, 0.0, 2.0, ALU.is_ge, ALU.mult))
                then(dve.scalar_tensor_tensor(size, g, -1.0, g, ALU.mult, ALU.max))
                then(dve.tensor_scalar(size, size, GATE_MIN, None, ALU.max))
                then(dve.tensor_scalar(sign, sign, -1.0, factor, ALU.add, ALU.mult))
                dve.tensor_tensor(g, sign, size, ALU.mult).then_inc(s_piece, 1)

            def cut_weight(what, pair, shape):
                half, landed = LANDED[what]
                dve.wait_ge(s_stage[half], landed)
                src = stage[:, half]
                src = src[:, 0, :] if shape == 1 else src[:, :, 0:shape]
                hi, lo = (w[:, :] if shape == 1 else w[:, :, :] for w in pair)
                then(dve.tensor_copy(hi, src))
                dve.tensor_tensor(lo, src, hi.bitcast(F32), ALU.subtract).then_inc(s_piece, 1)

            dve.sem_inc(s_rv, TPU)
            dve.sem_inc(s_out, TPU)
            dve.wait_ge(s_silu, 1)
            then(dve.tensor_scalar(silu_c[:, :, :], silu_c[:, :, :], EXP_CAP, 1.0, ALU.min, ALU.add))
            then(dve.reciprocal(silu_c[:, :, :], silu_c[:, :, :]))
            dve.wait_ge(s_const, 64)
            dve.tensor_tensor(silu_c[:, :, :], silu_c[:, :, :], c_in[:, :, :], ALU.mult).then_inc(s_silu, 1)
            run(normalise(0))
            columns("sa", tab_h[:, :, KC:2 * KC])
            columns("ca", tab_h[:, :, 0:KC])
            new_columns(0, tab_h, cur_h, s_cur_h)
            cut_weight("proj", proj, 256)
            run(h_high(0, 0), normalise(1))
            gate("ga", 0, 1.0)
            cut_weight("wd", wd, D)
            cut_weight("wc", wc, 1)
            run(recurrence_up(0, 0, True), recurrence_down(0), h_high(1, 1))
            states_high(0)
            run(normalise(2))
            columns("sb", tab_m[:, :, SHIFT:SHIFT + KC])
            columns("cb", cb1[:, :, :])
            then(dve.tensor_scalar(one_minus_mu[:, :, :], mu[:, :, :], -1.0, 1.0, ALU.mult, ALU.add))
            shift = tab_m[:, :, SHIFT:SHIFT + KC]
            for at, a, col in ((A_R, cb1, mu[:, 0:1, :]), (A_K, cb1, mu[:, 1:2, :]),
                               (B_R, cb1, one_minus_mu[:, 0:1, :]), (B_K, cb1, one_minus_mu[:, 1:2, :]),
                               (FIRST_R, None, mu[:, 0:1, :]), (FIRST_K, None, mu[:, 1:2, :])):
                src = shift if a is None else a[:, :, :]
                then(dve.tensor_tensor(tab_m[:, :, at:at + KC], src, col.broadcast_to([P, B, KC]), ALU.mult))
            new_columns(0, tab_m, cur_m, s_cur_m)
            gate("gb", 1, 0.5)
            cut_weight("wk", wk, D)
            cut_weight("wr", wr, D)
            cut_weight("wv", wv, D)
            run(residual(0, 0, True), recurrence_up(1, 1, False), normalise2(0, 0), mixes(0, 0, True),
                mix_r_high(0, True), residual(0, 1, False), normalise2(0, 1), h_high(2, 0))

            def slots(b, last):
                up = iter(())
                for s in range(UPB):
                    u, q = b * UPB + s, b * CPB + s // 2
                    next_mix = not (last and s + 1 >= UPB)
                    next_cd = not (last and s + 2 >= UPB)
                    next_unit = (b + (s + 1) // UPB, (s + 1) % UPB)
                    cd_unit = (b + (s + 2) // UPB, (s + 2) % UPB)
                    if s + 1 == UPB and not last:
                        new_columns(b + 1, tab_m, cur_m, s_cur_m)
                    mix_steps = mixes(*next_unit, False) if next_mix else iter(())
                    if s % 2 == 0:
                        down = recurrence_down(q + 1) if next_cd else iter(())
                        take(down, 10)
                        beside(down, k_high(u), 2)
                        run(down)
                        take(mix_steps, 7)
                        if next_cd:
                            states_high(q + 1)
                        run(mix_steps)
                        if not (last and s // 2 + 2 >= CPB):
                            up = recurrence_up(q + 2, (s // 2 + 2) % CPB, False)
                        take(up, EVEN_SOLO)
                        if next_mix:
                            beside(up, mix_r_high(u + 1, False), 1)
                        if next_cd:
                            beside(up, residual(*cd_unit, False), 2)
                        if not (last and s // 2 + 3 >= CPB):
                            beside(up, normalise(q + 3), 1)
                        if next_cd:
                            beside(up, normalise2(*cd_unit), 1)
                        beside(up, output(b, s), 1)
                    else:
                        if s // 2 + 3 == CPB and not last:
                            new_columns(b + 1, tab_h, cur_h, s_cur_h)
                        take(up, ODD_SOLO)
                        beside(up, k_high(u), 2)
                        beside(up, mix_steps, 1)
                        if next_cd:
                            beside(up, residual(*cd_unit, False), 2)
                        if not (last and s // 2 + 3 >= CPB):
                            beside(up, h_high(q + 3, (s // 2 + 3) % 2), 1)
                        if next_cd:
                            beside(up, normalise2(*cd_unit), 1)
                        if next_mix:
                            beside(up, mix_r_high(u + 1, False), 1)
                        beside(up, output(b, s), 2)
                        run(up)

            with dve.Fori(0, B - 1) as b:
                slots(b, False)
            slots(B - 1, True)

        @block.gpsimd
        def _(pool):
            def low(out, full, high, s_low):
                pool.tensor_tensor(out, full, high.bitcast(F32), ALU.subtract).then_inc(s_low, 1)

            def rstd_of(sq, var, rstd, index, s_sq, s_var, s_rstd):
                n = sq.shape[1]
                pool.wait_ge(s_sq, index * n + n)
                pool.tensor_tensor(var[:, :], sq[:, :], inv_d[:, 0:n], ALU.mult).then_inc(s_var, 1)
                pool.wait_ge(s_var, index * 2 + 1)
                pool.tensor_tensor(var[:, :], var[:, :], eps[:, 0:n], ALU.add).then_inc(s_var, 1)
                pool.wait_ge(s_var, index * 2 + 2)
                pool.tensor_tensor(rstd[:, :], var[:, :], minus_half[:, 0:n], ALU.pow).then_inc(s_rstd, 1)

            def rstd1_of(q):
                rstd_of(sq1, var1, rstd1, q, s_sq1, s_var1, s_rstd1)

            def rstd2_of(u):
                rstd_of(sq2, var2, rstd2, u, s_sq2, s_var2, s_rstd2)

            def h_low(q, par):
                for k in range(KC):
                    pool.wait_ge(s_h_hi, q * KC + k + 1)
                    low(h[par][1][:, k, :], h_full[:, k, :], h[par][0][:, k, :], s_h_lo)

            def states_low(q):
                pool.wait_ge(s_xs_hi, q + 1)
                low(xss[1][:, :], xs[:, :], xss[0][:, :], s_xs_lo)

            def mix_low(u, n):
                for j in range(2):
                    k = slice(2 * j, 2 * j + 2)
                    pool.wait_ge(s_mix_hi[n], u * 2 + j + 1)
                    low(mixs[n][1][:, k, :], mix[n][:, k, :], mixs[n][0][:, k, :], s_mix_lo[n])

            def add_output(u, place):
                for i in range(TPU):
                    pool.wait_ge(s_rvg, u * TPU + i + 1)
                    pool.tensor_tensor(x2[:, place, i, :], x2[:, place, i, :], rt[:, i, :], ALU.add).then_inc(s_out, 1)

            def k_low(u):
                for i in range(2):
                    pool.wait_ge(s_kk_hi, u * 2 + i + 1)
                    k = slice(2 * i, 2 * i + 2)
                    low(kks[1][:, k, :], kk[:, i, :].rearrange("p (c t) -> p c t", c=2), kks[0][:, k, :], s_kk_lo)

            for c, value in ((inv_d, 1.0 / D), (eps, EPS), (minus_half, -0.5)):
                pool.memset(c[:, :], value).then_inc(s_pool_const, 1)
            pool.wait_ge(s_pool_const, 3)
            rstd1_of(0)
            h_low(0, 0)
            rstd1_of(1)
            h_low(1, 1)
            states_low(0)
            rstd1_of(2)
            rstd2_of(0)
            mix_low(0, 0)
            mix_low(0, 1)
            rstd2_of(1)
            h_low(2, 0)

            def slots(b, last):
                for s in range(UPB):
                    u, q = b * UPB + s, b * CPB + s // 2
                    next_mix, next_cd = not (last and s + 1 >= UPB), not (last and s + 2 >= UPB)
                    k_low(u)
                    if next_mix:
                        mix_low(u + 1, 0)
                    if s % 2 == 0:
                        if next_cd:
                            states_low(q + 1)
                        if next_mix:
                            mix_low(u + 1, 1)
                        if not (last and s // 2 + 3 >= CPB):
                            rstd1_of(q + 3)
                        if next_cd:
                            rstd2_of(u + 2)
                    else:
                        if next_cd:
                            rstd2_of(u + 2)
                        if not (last and s // 2 + 3 >= CPB):
                            h_low(q + 3, (s // 2 + 3) % 2)
                        if next_mix:
                            mix_low(u + 1, 1)
                    add_output(u, s % 4)

            with pool.Fori(0, B - 1) as b:
                slots(b, False)
            slots(B - 1, True)


def kernel(**inputs):
    import concourse.bacc as bacc
    from concourse.bass_utils import run_bass_kernel_spmd

    def a(name):
        return np.asarray(inputs["L0_" + name])

    def t(w):
        return np.ascontiguousarray(w.T)

    b_b = a("attn_b_B")
    arrays = {
        "x": a("attn_u").reshape(B * T, D),
        "c": np.ascontiguousarray(a("c").T.reshape(KC, P, B).transpose(1, 0, 2)),
        "ident": np.eye(P, dtype=np.float32),
        "scan_bias": np.ascontiguousarray(np.stack(
            [np.tile(v, 2) for v in (a("attn_b_omega"), a("attn_b_zeta"), b_b[:M], b_b[M:])], axis=1)),
        "mu": np.ascontiguousarray(np.stack(
            [a("ffn_mu_r").reshape(KC, P).T, a("ffn_mu_k").reshape(KC, P).T], axis=1)),
        "wmod": a("wmod"),
        "w_omega": t(a("attn_W_omega")), "w_zeta": t(a("attn_W_zeta")), "w_b": t(a("attn_W_B")),
        "wd": t(a("attn_D_mat")), "wc": t(a("attn_C")),
        "wk": t(a("ffn_W_k")), "wr": t(a("ffn_W_r")), "wv": t(a("ffn_W_v")),
    }
    arrays = {k: np.ascontiguousarray(v) for k, v in arrays.items()}
    nc = bacc.Bacc("TRN2", target_bir_lowering=False, num_devices=1, dynamic_dma_scratch_size=1024)
    dram = {k: nc.dram_tensor(f"in_{k}", v.shape, F32, kind="ExternalInput").ap() for k, v in arrays.items()}
    dram["gate_rows"] = nc.dram_tensor("gate_rows", [2, B, D], F32, kind="Internal").ap()
    dram["out"] = nc.dram_tensor("out", [B * T, D], F32, kind="ExternalOutput").ap()
    build(nc, dram)
    r = run_bass_kernel_spmd(nc, [{f"in_{k}": v for k, v in arrays.items()}], core_ids=[0])
    return np.asarray(r.results[0]["out"]).reshape(B, T, D)
```

```python
from contextlib import ExitStack

import numpy as np

import concourse.bass as bass
from concourse import mybir

F32 = mybir.dt.float32
F32R = mybir.dt.float32r
ALU = mybir.AluOpType
ACT = mybir.ActivationFunctionType

B, T, D, M = 4, 2048, 512, 64
P = 128
KC = D // P
CHUNK, UNIT, HALF = 512, 256, 256
CPB = T // CHUNK
UPB = T // UNIT
NCHUNK, NUNIT = B * CPB, B * UPB
TPU, TPC = UNIT // P, CHUNK // P
LEVELS = HALF.bit_length() - 1
DT, OMEGA_MIN, OMEGA_MAX, EPS, GATE_MIN = 0.01, 1e-4, 100.0, 1e-5, 0.25
EXP_CAP = 1e30
A_R, A_K, B_R, B_K, SHIFT, FIRST_R, FIRST_K, NTAB = 0, 4, 8, 12, 16, 20, 24, 28
STEP_NEG_ABS, STEP_COEFFS = 3, 11
STEP_TREE = STEP_COEFFS + 11 + 4 * (LEVELS - 1)
STEP_ROOTS = STEP_TREE + 8
STEPS = STEP_ROOTS + 3 * (LEVELS - 1) + 5
EVEN_SOLO, ODD_SOLO = 20, 8
SPLIT_LEVEL = 3
EDGES = 3 + 5 * (UPB - 1)


def build(nc, d):
    ctx = ExitStack()
    with ctx:
        def sb(name, shape, dt=F32):
            return ctx.enter_context(nc.sbuf_tensor(name, shape, dt))

        def sem(name):
            return ctx.enter_context(nc.semaphore(name))

        proj = [sb(f"proj_{n}", [P, KC, 256], F32R) for n in ("hi", "lo")]
        wd = [sb(f"wd_{n}", [P, KC, D], F32R) for n in ("hi", "lo")]
        wc = [sb(f"wc_{n}", [P, D], F32R) for n in ("hi", "lo")]
        wk = [sb(f"wk_{n}", [P, KC, D], F32R) for n in ("hi", "lo")]
        wr = [sb(f"wr_{n}", [P, KC, D], F32R) for n in ("hi", "lo")]
        wv = [sb(f"wv_{n}", [P, KC, D], F32R) for n in ("hi", "lo")]
        ident = sb("ident", [P, P])
        scan_bias = sb("scan_bias", [P, 4])
        mu = sb("mu", [P, 2, KC])
        one_minus_mu = sb("one_minus_mu", [P, 2, KC])
        silu_c = sb("silu_c", [P, KC, B])
        c_in = sb("c_in", [P, KC, B])
        tab_h = sb("tab_h", [P, B, 2 * KC])
        tab_m = sb("tab_m", [P, B, NTAB])
        cb1 = sb("cb1", [P, B, KC])
        cur_h = sb("cur_h", [P, 2 * KC])
        cur_m = sb("cur_m", [P, NTAB])
        gate_a = sb("gate_a", [P, D])
        gate_b = sb("gate_b", [P, D])
        inv_d, eps, minus_half = (sb(n, [P, TPC]) for n in ("inv_d", "eps", "minus_half"))

        x_in = sb("x_in", [P, TPC, D])
        sum1 = sb("sum1", [P, TPC])
        neg_mean1 = sb("neg_mean1", [P, TPC])
        sq1 = sb("sq1", [P, TPC])
        var1 = sb("var1", [P, TPC])
        square_out = sb("square_out", [P, 2, D], mybir.dt.bfloat16)
        rstd1 = sb("rstd1", [P, TPC])
        h_full = sb("h_full", [P, KC, CHUNK])
        h = [[sb(f"h_{n}{i}", [P, KC, CHUNK], F32R) for n in ("hi", "lo")] for i in range(2)]

        x2 = sb("x2", [P, 4, TPU, D])
        sum2 = sb("sum2", [P, TPU])
        neg_mean2 = sb("neg_mean2", [P, TPU])
        sq2 = sb("sq2", [P, TPU])
        var2 = sb("var2", [P, TPU])
        rstd2 = sb("rstd2", [P, TPU])
        xn2 = sb("xn2", [P, TPU, D])
        last_n = sb("last_n", [P, KC])
        mix_full = sb("mix_full", [P, 2, KC, UNIT])
        mix = [mix_full[:, n] for n in range(2)]
        mixs = [[sb(f"mix_{n}_{w}", [P, KC, UNIT], F32R) for w in ("hi", "lo")] for n in "kr"]
        kk = sb("kk", [P, 2, 2 * UNIT])
        kks = [sb(f"kk_{m}", [P, KC, UNIT], F32R) for m in ("hi", "lo")]
        rt = sb("rt", [P, TPU, D])

        om = sb("om", [P, HALF])
        om_pos = sb("om_pos", [P, HALF])
        om_exp = sb("om_exp", [P, HALF])
        ze = sb("ze", [P, HALF])
        hh = sb("hh", [P, HALF])
        ee = sb("ee", [P, HALF])
        f0 = sb("f0", [P, 2, HALF])
        tree = [None] + [sb(f"tree{l}", [P, 2, 3, HALF >> l]) for l in range(1, LEVELS + 1)]
        tmp0 = sb("tmp0", [P, 384])
        tmp1 = sb("tmp1", [P, 384])
        state = sb("state", [P, 2, HALF + 1])
        xs = sb("xs", [P, CHUNK])
        xss = [sb(f"xs_{m}", [P, CHUNK], F32R) for m in ("hi", "lo")]

        stage = [x2[:, 0:2].rearrange("p a t n -> p (a t) n"), x2[:, 2:4].rearrange("p a t n -> p (a t) n"),
                 mix_full[:, :].rearrange("p a k t -> p (a k t)").rearrange("p (k n) -> p k n", k=KC),
                 xs[:, :].unsqueeze(1)]

        def banks(name):
            return ctx.enter_context(nc.psum_tensor(name, [P, 2, 512], F32))

        ps_kr, ps_tv, ps_pt, ps_cd = banks("ps_kr"), banks("ps_tv"), banks("ps_pt"), banks("ps_cd")

        s_const = sem("s_const")
        s_stage = [sem(f"s_stage{i}") for i in range(len(stage))]
        s_cut_hi, s_cut = sem("s_cut_hi"), sem("s_cut")
        s_mod = sem("s_mod")
        s_row = sem("s_row")
        s_cols = sem("s_cols")
        s_tab_h, s_tab_m = sem("s_tab_h"), sem("s_tab_m")
        s_gate = sem("s_gate")
        s_prep = sem("s_prep")
        s_silu = sem("s_silu")
        s_rows = sem("s_rows")
        s_gate_a, s_gate_b = sem("s_gate_a"), sem("s_gate_b")
        s_pool_const = sem("s_pool_const")
        s_cur_h, s_cur_m = sem("s_cur_h"), sem("s_cur_m")
        s_xin = sem("s_xin")
        s_sum1 = sem("s_sum1")
        s_mean1 = sem("s_mean1")
        s_sq1 = sem("s_sq1")
        s_var1 = sem("s_var1")
        s_rstd1 = sem("s_rstd1")
        s_xn1 = sem("s_xn1")
        s_t1 = sem("s_t1")
        s_h = sem("s_h")
        s_h_hi, s_h_lo = sem("s_h_hi"), sem("s_h_lo")
        s_p = sem("s_p")
        s_pev = sem("s_pev")
        s_zexp = sem("s_zexp")
        s_wexp = sem("s_wexp")
        s_softln = sem("s_softln")
        s_rec = sem("s_rec")
        s_xs = sem("s_xs")
        s_xs_hi, s_xs_lo = sem("s_xs_hi"), sem("s_xs_lo")
        s_x2in = [sem(f"s_x2in{r}") for r in range(4)]
        s_cd = sem("s_cd")
        s_gated = sem("s_gated")
        s_x2 = sem("s_x2")
        s_mean2, s_sq2, s_var2 = sem("s_mean2"), sem("s_sq2"), sem("s_var2")
        s_rstd2 = sem("s_rstd2")
        s_xn2 = sem("s_xn2")
        s_t2 = sem("s_t2")
        s_prev = sem("s_prev")
        s_edge = sem("s_edge")
        s_mix = sem("s_mix")
        s_mix_hi = [sem("s_mix_k_hi"), sem("s_mix_r_hi")]
        s_mix_lo = [sem("s_mix_k_lo"), sem("s_mix_r_lo")]
        s_k, s_r, s_v = sem("s_k"), sem("s_r"), sem("s_v")
        s_relu, s_kk = sem("s_relu"), sem("s_kk")
        s_kk_hi, s_kk_lo = sem("s_kk_hi"), sem("s_kk_lo")
        s_rt = sem("s_rt")
        s_rv = sem("s_rv")
        s_rvg = sem("s_rvg")
        s_out = sem("s_out")
        s_stored = sem("s_stored")

        x_rows = d["x"].rearrange("(q i p) n -> q p i n", p=P, i=TPC)
        x_units = d["x"].rearrange("(u i p) n -> u p i n", p=P, i=TPU)
        out_units = d["out"].rearrange("(u i p) n -> u p i n", p=P, i=TPU)
        rows = d["gate_rows"]

        def mod_piece(v):
            return d["wmod"][:, v * D:(v + 1) * D].rearrange("(k p) n -> p k n", p=P)

        def weight_piece(name):
            return d[name].rearrange("(k p) n -> p k n", p=P)

        PIECES = {"sa": 0, "ca": 1, "proj": 2, "wc": 3, "wd": 0, "ga": 1, "sb": 2, "gb": 1, "wr": 2, "cb": 0,
                  "wv": 1, "wk": 0}
        MOD_PART = {"sa": 0, "ca": 1, "ga": 2, "sb": 3, "cb": 4, "gb": 5}
        MODS = [p for p in PIECES if p in MOD_PART]
        WEIGHTS = {"proj": proj, "wd": wd, "wc": wc, "wk": wk, "wr": wr, "wv": wv}
        CUTS = [p for p in PIECES if p in WEIGHTS]
        LANDED, FORMER, landed, owner = {}, {}, {}, {}
        for what, place in PIECES.items():
            landed[place] = landed.get(place, 0) + 16 * (3 if what == "proj" else 1)
            LANDED[what] = landed[place]
            FORMER[what] = owner.get(place)
            owner[place] = what

        def weight_views(what):
            hi, lo = WEIGHTS[what]
            src = stage[PIECES[what]]
            if what == "wc":
                return hi[:, :], lo[:, :], src[:, 0, :]
            return hi[:, :, :], lo[:, :, :], src[:, :, 0:hi.shape[2]]

        block = ctx.enter_context(nc.Block())

        @block.sync
        def _(sp):
            sp.dma_start(c_in[:, :, :], d["c"]).then_inc(s_const, 16)
            sp.dma_start(x_in[:, :, :], x_rows[0]).then_inc(s_xin, 16)
            sp.dma_start(ident[:, :], d["ident"]).then_inc(s_const, 16)
            sp.dma_start(scan_bias[:, :], d["scan_bias"]).then_inc(s_const, 16)
            sp.dma_start(mu[:, :, :], d["mu"]).then_inc(s_const, 16)
            for what, place in PIECES.items():
                former = FORMER[what]
                if former in MODS:
                    sp.wait_ge(s_mod, MODS.index(former) + 1)
                elif former:
                    sp.wait_ge(s_cut, CUTS.index(former) + 1)
                st, s = stage[place], s_stage[place]
                if what in MODS:
                    sp.dma_start(st, mod_piece(MOD_PART[what])).then_inc(s, 16)
                elif what == "proj":
                    for name, at, w in (("w_omega", 0, M), ("w_zeta", M, M), ("w_b", 2 * M, 2 * M)):
                        sp.dma_start(st[:, :, at:at + w], weight_piece(name)).then_inc(s, 16)
                elif what == "wc":
                    sp.dma_start(st[:, 0, :], d["wc"]).then_inc(s, 16)
                else:
                    sp.dma_start(st, weight_piece(what)).then_inc(s, 16)
                if what in ("ga", "wv"):
                    q = 1 if what == "ga" else 2
                    sp.wait_ge(s_t1, q * KC)
                    sp.dma_start(x_in[:, :, :], x_rows[q]).then_inc(s_xin, 16)
            sp.wait_ge(s_gate, 2)
            sp.dma_start(rows[0], xn2[0:B, 0, :]).then_inc(s_rows, 16)
            sp.dma_start(rows[1], xn2[0:B, 1, :]).then_inc(s_rows, 16)
            sp.wait_ge(s_rows, 32)
            sp.dma_start(gate_a[:, :], rows[0, 0:1, :].partition_broadcast(P)).then_inc(s_gate_a, 16)
            sp.dma_start(gate_b[:, :], rows[1, 0:1, :].partition_broadcast(P)).then_inc(s_gate_b, 16)
            sp.wait_ge(s_cut, len(CUTS))
            for u in range(3):
                sp.dma_start(x2[:, u], x_units[u]).then_inc(s_x2in[u], 16)
            sp.sem_inc(s_stored, 16)

            def slots(b, last):
                for s in range(UPB):
                    u = b * UPB + s
                    if s == 6 and not last:
                        sp.wait_ge(s_gated, (b + 1) * (UPB * TPU))
                        sp.dma_start(gate_a[:, :], rows[0, bass.ds(b + 1, 1), :].partition_broadcast(P))\
                          .then_inc(s_gate_a, 16)
                    if not (last and s + 3 >= UPB):
                        sp.wait_ge(s_stored, u * 16 + 16)
                        sp.dma_start(x2[:, (s + 3) % 4], x_units[u + 3]).then_inc(s_x2in[(s + 3) % 4], 16)
                    if s % 2 == 0 and not (last and s // 2 + 3 >= CPB):
                        q = b * CPB + s // 2 + 3
                        sp.wait_ge(s_t1, q * KC)
                        sp.dma_start(x_in[:, :, :], x_rows[q]).then_inc(s_xin, 16)
                    sp.wait_ge(s_out, u * TPU + 2 * TPU)
                    sp.dma_start(out_units[u], x2[:, s % 4]).then_inc(s_stored, 16)
                if not last:
                    sp.dma_start(gate_b[:, :], rows[1, bass.ds(b + 1, 1), :].partition_broadcast(P))\
                      .then_inc(s_gate_b, 16)

            with sp.Fori(0, B - 1) as b:
                slots(b, False)
            slots(B - 1, True)
            sp.wait_ge(s_stored, 16 * (NUNIT + 1))

        @block.tensor
        def _(pe):
            def product(out, act, weight, acc0=True, acc1=True):
                n = len(act[0])
                mm = None
                for a, w in ((0, 0), (0, 1), (1, 0)):
                    for k in range(n):
                        mm = pe.matmul(out, act[a][k], weight[w][k],
                                       start=acc0 and a == 0 and w == 0 and k == 0,
                                       stop=acc1 and a == 1 and k == n - 1)
                return mm

            def t1_blocks(q, ks):
                for k in ks:
                    for i in range(TPC):
                        mm = pe.transpose(ps_pt[:, k % 2, i * P:(i + 1) * P],
                                          x_in[:, i, k * P:(k + 1) * P], ident[:, :])
                    mm.then_inc(s_t1, 1)

            def projections(q, par):
                pe.wait_ge(s_h_hi, q * KC + KC)
                pe.wait_ge(s_h_lo, q * KC + KC)
                for m in range(2):
                    product(ps_pt[:, m, :],
                            [[proj[w][:, k, m * P:(m + 1) * P] for k in range(KC)] for w in range(2)],
                            [[h[par][w][:, k, :] for k in range(KC)] for w in range(2)]).then_inc(s_p, 1)

            def h_part(s, banks, tiles=range(TPU)):
                par, at = (s // 2) % 2, (s % 2) * UNIT
                for i in tiles:
                    t = slice(at + i * P, at + (i + 1) * P)
                    product(banks[:, i, :], [[h[par][w][:, k, t] for k in range(KC)] for w in range(2)],
                            [[wd[w][:, k, :] for k in range(KC)] for w in range(2)], acc1=False)

            def states_part(s, banks, tiles=range(TPU)):
                for i in tiles:
                    t = slice((s % 2) * UNIT + i * P, (s % 2) * UNIT + (i + 1) * P)
                    product(banks[:, i, :], [[xss[w][:, t]] for w in range(2)],
                            [[wc[w][:, :]] for w in range(2)], acc0=False).then_inc(s_cd, 1)

            def t2_blocks(u):
                pe.wait_ge(s_xn2, u * TPU + TPU)
                for k in range(KC):
                    for i in range(TPU):
                        at = (k % 2) * UNIT + i * P
                        mm = pe.transpose(ps_tv[:, k // 2, at:at + P], xn2[:, i, k * P:(k + 1) * P],
                                          ident[:, :])
                    mm.then_inc(s_t2, 1)

            def modulation(what):
                n = MODS.index(what)
                pe.wait_ge(s_stage[PIECES[what]], LANDED[what])
                if n >= 2:
                    pe.wait_ge(s_row, n - 1)
                w = stage[PIECES[what]]
                for k in range(KC):
                    mm = pe.matmul(ps_cd[0:B, n % 2, :], silu_c[:, k, :], w[:, k, :],
                                   start=(k == 0), stop=(k == KC - 1))
                mm.then_inc(s_mod, 1)

            def row_to_columns(what, n):
                pe.wait_ge(s_row, MODS.index(what) + 1)
                if n >= 2:
                    pe.wait_ge(s_tab_h, 1)
                for k in range(KC):
                    mm = pe.transpose(ps_tv[:, n % 2, k * B:(k + 1) * B], rt[0:B, n % 2, k * P:(k + 1) * P],
                                      ident[0:B, 0:B])
                mm.then_inc(s_cols, 1)

            def rest_transposed_in(q):
                for k in (2, 3):
                    pe.wait_ge(s_h, q * KC + k - 1)
                    t1_blocks(q, (k,))

            pe.wait_ge(s_const, 64)
            pe.wait_ge(s_silu, 2)
            modulation("sa")
            modulation("ca")
            pe.wait_ge(s_xn1, TPC)
            t1_blocks(0, (0, 1))
            row_to_columns("sa", 0)
            row_to_columns("ca", 1)
            rest_transposed_in(0)
            pe.wait_ge(s_h, KC)
            pe.wait_ge(s_cut, CUTS.index("proj") + 1)
            projections(0, 0)
            modulation("ga")
            modulation("sb")
            modulation("gb")
            modulation("cb")
            row_to_columns("sb", 2)
            row_to_columns("cb", 3)
            pe.wait_ge(s_pev, 1)
            pe.wait_ge(s_xn1, 2 * TPC)
            t1_blocks(1, (0, 1))
            rest_transposed_in(1)
            pe.wait_ge(s_h, 2 * KC)
            projections(1, 1)
            pe.wait_ge(s_cut, CUTS.index("wd") + 1)
            pe.wait_ge(s_row, len(MODS))
            h_part(0, ps_cd)
            h_part(1, ps_kr)
            pe.wait_ge(s_xs_hi, 1)
            pe.wait_ge(s_xs_lo, 1)
            states_part(0, ps_cd)
            states_part(1, ps_kr)
            pe.wait_ge(s_pev, 2)
            pe.wait_ge(s_xn1, 3 * TPC)
            t1_blocks(2, (0, 1))
            pe.wait_ge(s_tab_m, 1)
            t2_blocks(0)
            rest_transposed_in(2)

            def k_product(u):
                pe.wait_ge(s_mix_hi[0], u * 2 + 2)
                pe.wait_ge(s_mix_lo[0], u * 2 + 2)
                pe.wait_ge(s_rt, u * TPU + TPU)
                for m in range(KC):
                    mm = product(ps_kr[:, m // 2, (m % 2) * UNIT:(m % 2 + 1) * UNIT],
                                 [[wk[w][:, k, m * P:(m + 1) * P] for k in range(KC)] for w in range(2)],
                                 [[mixs[0][w][:, k, :] for k in range(KC)] for w in range(2)])
                    if m % 2:
                        mm.then_inc(s_k, 1)

            def r_product(u):
                pe.wait_ge(s_mix_hi[1], u * 2 + 2)
                pe.wait_ge(s_mix_lo[1], u * 2 + 2)
                pe.wait_ge(s_relu, u * 2 + 2)
                for i in range(TPU):
                    product(ps_kr[:, i, :],
                            [[mixs[1][w][:, k, i * P:(i + 1) * P] for k in range(KC)] for w in range(2)],
                            [[wr[w][:, k, :] for k in range(KC)] for w in range(2)]).then_inc(s_r, 1)

            def v_product(u, mixes_before):
                pe.wait_ge(s_kk_hi, u * 2 + 2)
                pe.wait_ge(s_kk_lo, u * 2 + 2)
                if mixes_before:
                    pe.wait_ge(s_mix, u * 2 * KC + 4 * KC)
                else:
                    pe.wait_ge(s_rv, u * TPU + TPU)
                for i in range(TPU):
                    product(ps_tv[:, i, :],
                            [[kks[w][:, k, i * P:(i + 1) * P] for k in range(KC)] for w in range(2)],
                            [[wv[w][:, k, :] for k in range(KC)] for w in range(2)]).then_inc(s_v, 1)

            def slots(b, last):
                for s in range(UPB):
                    u, q = b * UPB + s, b * CPB + s // 2
                    t1 = s % 2 == 1 and not (last and s // 2 + 3 >= CPB)
                    if s == 0:
                        pe.wait_ge(s_cut, len(CUTS))
                        pe.wait_ge(s_gated, 2 * TPU)
                    k_product(u)
                    if t1:
                        pe.wait_ge(s_xn1, q * TPC + 4 * TPC)
                        pe.wait_ge(s_pev, q + 3)
                        t1_blocks(q + 3, (0, 1))
                    t2 = not (last and s + 1 >= UPB)
                    cd = not (last and s + 2 >= UPB)
                    if t2 and (s % 2 == 0 or not cd):
                        pe.wait_ge(s_rv, u * TPU + TPU)
                        t2_blocks(u + 1)
                    if s % 2 == 0:
                        if not (last and s // 2 + 2 >= CPB):
                            pe.wait_ge(s_h, q * KC + 3 * KC)
                            projections(q + 2, (s // 2) % 2)
                        r_product(u)
                    if cd:
                        pe.wait_ge(s_gated, u * TPU + 2 * TPU)
                        place = (s + 2) % UPB
                        if s % 2 == 0:
                            h_part(place, ps_cd)
                            pe.wait_ge(s_xs_hi, q + 2)
                            pe.wait_ge(s_xs_lo, q + 2)
                            states_part(place, ps_cd)
                        else:
                            h_part(place, ps_cd, (0,))
                            states_part(place, ps_cd, (0,))
                            pe.wait_ge(s_rv, u * TPU + TPU)
                            t2_blocks(u + 1)
                            h_part(place, ps_cd, (1,))
                            states_part(place, ps_cd, (1,))
                    if t1:
                        for k in (2, 3):
                            pe.wait_ge(s_h, q * KC + 3 * KC + k - 1)
                            t1_blocks(q + 3, (k,))
                    if s % 2 == 1:
                        r_product(u)
                    v_product(u, not (last and s + 1 >= UPB))

            with pe.Fori(0, B - 1) as b:
                slots(b, False)
            slots(B - 1, True)

        @block.scalar
        def _(act):
            def h_blocks(q, ks):
                for k in ks:
                    act.wait_ge(s_t1, q * KC + k + 1)
                    act.activation(h_full[:, k, :], ps_pt[:, k % 2, :], ACT.Identity,
                                   bias=cur_h[:, KC + k:KC + k + 1], scale=cur_h[:, k:k + 1]).then_inc(s_h, 1)

            def squares(x, neg_mean, out, count, s_sq):
                for i in range(out.shape[1]):
                    if i >= 2:
                        act.wait_ge(s_sq, count + i - 1)
                    act.activation(square_out[:, i % 2, :], x[:, i, :], ACT.Square, bias=neg_mean[:, i:i + 1],
                                   accum_out=out[:, i:i + 1]).then_inc(s_sq, 1)

            def statistics1(q):
                act.wait_ge(s_xin, q * 16 + 16)
                for i in range(TPC):
                    act.activation(x_in[:, i, :], x_in[:, i, :], ACT.Identity, accum_out=sum1[:, i:i + 1])\
                       .then_inc(s_sum1, 1)
                act.wait_ge(s_sum1, q * TPC + TPC)
                act.activation(neg_mean1[:, :], sum1[:, :], ACT.Identity, scale=-1.0 / D).then_inc(s_mean1, 1)
                act.wait_ge(s_mean1, q + 1)
                squares(x_in, neg_mean1, sq1, q * TPC, s_sq1)

            def statistics2(b, s):
                u = b * UPB + s
                act.wait_ge(s_x2, u * TPU + TPU)
                act.activation(neg_mean2[:, :], sum2[:, :], ACT.Identity, scale=-1.0 / D).then_inc(s_mean2, 1)
                act.wait_ge(s_mean2, u + 1)
                squares(x2[:, s % 4], neg_mean2, sq2, u * TPU, s_sq2)

            def projections_out(q):
                act.wait_ge(s_p, q * 2 + 2)
                for half in range(2):
                    to, cols = slice(half * M, half * M + M), slice(half * HALF, (half + 1) * HALF)
                    act.activation(om[to, :], ps_pt[0:M, 0, cols], ACT.Identity)
                    act.activation(ze[to, :], ps_pt[M:2 * M, 0, cols], ACT.Identity)
                    act.activation(f0[to, 0, :], ps_pt[0:M, 1, cols], ACT.Identity)
                    mm = act.activation(f0[to, 1, :], ps_pt[M:2 * M, 1, cols], ACT.Identity)
                mm.then_inc(s_pev, 1)

            def softplus_parts(q):
                act.wait_ge(s_pev, q + 1)
                act.activation(ze[:, :], ze[:, :], ACT.Exp, bias=scan_bias[:, 1:2]).then_inc(s_zexp, 1)
                act.wait_ge(s_rec, q * STEPS + STEP_NEG_ABS)
                act.activation(om_exp[:, :], om_exp[:, :], ACT.Exp).then_inc(s_wexp, 1)
                act.wait_ge(s_wexp, q + 1)
                act.activation(om_exp[:, :], om_exp[:, :], ACT.Ln, bias=1.0).then_inc(s_softln, 1)

            def states_out(q, first):
                act.wait_ge(s_rec, q * STEPS + STEPS)
                if not first:
                    act.wait_ge(s_xs_hi, q)
                    act.wait_ge(s_xs_lo, q)
                for half in range(2):
                    frm, cols = slice(half * M, half * M + M), slice(half * HALF, (half + 1) * HALF)
                    act.activation(xs[0:M, cols], state[frm, 0, 1:HALF + 1], ACT.Identity)
                    mm = act.activation(xs[M:2 * M, cols], state[frm, 1, 1:HALF + 1], ACT.Identity, scale=DT)
                mm.then_inc(s_xs, 1)

            def shifted(u, first):
                if not first:
                    for n in range(2):
                        act.wait_ge(s_mix_hi[n], u * 2)
                        act.wait_ge(s_mix_lo[n], u * 2)
                for j in range(2):
                    act.wait_ge(s_t2, u * KC + 2 * j + 2)
                    for n, beta in ((0, B_K), (1, B_R)):
                        for c in range(2):
                            k = 2 * j + c
                            mm = act.activation(mix[n][:, k, 1:UNIT], ps_tv[:, j, c * UNIT:(c + 1) * UNIT - 1],
                                                ACT.Identity, bias=cur_m[:, SHIFT + k:SHIFT + k + 1],
                                                scale=cur_m[:, beta + k:beta + k + 1])
                    mm.then_inc(s_prev, 1)

            def weight_high(what):
                act.wait_ge(s_stage[PIECES[what]], LANDED[what])
                hi, _, src = weight_views(what)
                act.activation(hi, src, ACT.Identity).then_inc(s_cut_hi, 1)

            def row_out(what, row):
                act.wait_ge(s_mod, MODS.index(what) + 1)
                act.activation(row, ps_cd[0:B, MODS.index(what) % 2, :], ACT.Identity).then_inc(s_row, 1)

            act.sem_inc(s_rt, TPU)
            act.wait_ge(s_const, 64)
            act.activation(silu_c[:, :, :], c_in[:, :, :], ACT.Exp, scale=-1.0).then_inc(s_silu, 1)
            statistics1(0)
            weight_high("proj")
            row_out("sa", rt[0:B, 0, :])
            row_out("ca", rt[0:B, 1, :])
            act.wait_ge(s_cur_h, 1)
            h_blocks(0, range(KC))
            weight_high("wc")
            weight_high("wd")
            projections_out(0)
            softplus_parts(0)
            row_out("ga", xn2[0:B, 0, :])
            statistics1(1)
            act.wait_ge(s_cols, 2)
            row_out("sb", rt[0:B, 0, :])
            row_out("gb", xn2[0:B, 1, :])
            row_out("cb", rt[0:B, 1, :])
            act.wait_ge(s_h_hi, KC)
            act.wait_ge(s_h_lo, KC)
            h_blocks(1, range(KC))
            weight_high("wr")
            weight_high("wv")
            weight_high("wk")
            statistics1(2)
            states_out(0, True)
            projections_out(1)
            statistics2(0, 0)
            softplus_parts(1)
            act.wait_ge(s_h_hi, 2 * KC)
            act.wait_ge(s_h_lo, 2 * KC)
            h_blocks(2, (0, 1))
            act.wait_ge(s_cur_m, 1)
            act.wait_ge(s_cut, len(CUTS))
            shifted(0, True)
            h_blocks(2, (2, 3))
            act.wait_ge(s_xn2, TPU)
            statistics2(0, 1)

            def slots(b, last):
                for s in range(UPB):
                    u = b * UPB + s
                    q = b * CPB + s // 2
                    act.wait_ge(s_rv, u * TPU + TPU)
                    for i in range(2):
                        act.wait_ge(s_k, u * 2 + i + 1)
                        act.activation(kk[:, i, :], ps_kr[:, i, :], ACT.Relu).then_inc(s_relu, 1)
                    for i in range(2):
                        act.wait_ge(s_relu, u * 2 + i + 1)
                        act.activation(kk[:, i, :], kk[:, i, :], ACT.Square).then_inc(s_kk, 1)
                    t1 = s % 2 == 1 and not (last and s // 2 + 3 >= CPB)
                    if t1:
                        if s // 2 + 3 == CPB:
                            act.wait_ge(s_cur_h, b + 2)
                        act.wait_ge(s_h_hi, q * KC + 3 * KC)
                        act.wait_ge(s_h_lo, q * KC + 3 * KC)
                        h_blocks(q + 3, (0, 1))
                    if not (last and s + 1 >= UPB):
                        if s + 1 == UPB:
                            act.wait_ge(s_cur_m, b + 2)
                        shifted(u + 1, False)
                    if s % 2 == 0 and not (last and s + 2 >= UPB):
                        states_out(q + 1, False)
                    p = s % 2 == 0 and not (last and s // 2 + 2 >= CPB)
                    if p:
                        projections_out(q + 2)
                    if t1:
                        h_blocks(q + 3, (2, 3))
                    if s % 2 == 1 and not (last and s + 2 >= UPB):
                        statistics2(b + (s + 2) // UPB, (s + 2) % UPB)
                    act.wait_ge(s_out, u * TPU + TPU)
                    for i in range(TPU):
                        act.wait_ge(s_r, u * TPU + i + 1)
                        act.activation(rt[:, i, :], ps_kr[:, i, :], ACT.Tanh, scale=0.5).then_inc(s_rt, 1)
                    if p:
                        softplus_parts(q + 2)
                    if s % 2 == 0 and not (last and s // 2 + 3 >= CPB):
                        statistics1(q + 3)
                    if s % 2 == 0 and not (last and s + 2 >= UPB):
                        statistics2(b + (s + 2) // UPB, (s + 2) % UPB)

            with act.Fori(0, B - 1) as b:
                slots(b, False)
            slots(B - 1, True)

        @block.vector
        def _(dve):
            def normalise(q):
                dve.wait_ge(s_rstd1, q + 1)
                for i in range(TPC):
                    dve.tensor_scalar(x_in[:, i, :], x_in[:, i, :], neg_mean1[:, i:i + 1], rstd1[:, i:i + 1],
                                      ALU.add, ALU.mult).then_inc(s_xn1, 1)
                    yield

            def h_high(q, par):
                if not (isinstance(q, int) and q < 2):
                    dve.wait_ge(s_cd, q * TPC - TPC)
                for k in range(KC):
                    dve.wait_ge(s_h, q * KC + k + 1)
                    dve.tensor_copy(h[par][0][:, k, :], h_full[:, k, :]).then_inc(s_h_hi, 1)
                    yield

            def states_high(q):
                dve.wait_ge(s_xs, q + 1)
                dve.tensor_copy(xss[0][:, :], xs[:, :]).then_inc(s_xs_hi, 1)

            def new_columns(b, table, cur, s_cur):
                dve.tensor_copy(cur[:, :], table[:, b, :] if isinstance(b, int)
                                else table[:, bass.ds(b, 1), :].rearrange("p a n -> p (a n)")).then_inc(s_cur, 1)

            def mixes(b, s, first):
                u = b * UPB + s
                at = b * EDGES + (0 if s == 0 else 3 + 5 * (s - 1))
                if s == 0:
                    dve.wait_ge(s_cur_m, b + 1)
                if not first:
                    for n in range(2):
                        dve.wait_ge(s_mix_lo[n], u * 2)
                cols = [mix[n][:, :, 0] for n in range(2)]
                if s == 0:
                    dve.tensor_copy(cols[0], cur_m[:, FIRST_K:FIRST_K + KC]).then_inc(s_edge, 1)
                    dve.tensor_copy(cols[1], cur_m[:, FIRST_R:FIRST_R + KC]).then_inc(s_edge, 1)
                    n_edges = 3
                else:
                    dve.tensor_tensor(cols[0], last_n[:, :], cur_m[:, B_K:B_K + KC], ALU.mult).then_inc(s_edge, 1)
                    dve.tensor_tensor(cols[1], last_n[:, :], cur_m[:, B_R:B_R + KC], ALU.mult).then_inc(s_edge, 1)
                    yield
                    for n in range(2):
                        dve.wait_ge(s_edge, at + n + 1)
                        dve.tensor_tensor(cols[n], cols[n], cur_m[:, SHIFT:SHIFT + KC], ALU.add).then_inc(s_edge, 1)
                    n_edges = 5
                yield
                dve.wait_ge(s_edge, at + n_edges - 1)
                for j in range(2):
                    dve.wait_ge(s_prev, u * 2 + j + 1)
                    if j == 1:
                        dve.tensor_copy(last_n[:, :],
                                        ps_tv[:, :, :].rearrange("p a (c t) -> p (a c) t", c=2)[:, :, UNIT - 1])\
                           .then_inc(s_edge, 1)
                        yield
                    for n, alpha in ((0, A_K), (1, A_R)):
                        for c in range(2):
                            k = 2 * j + c
                            dve.scalar_tensor_tensor(mix[n][:, k, :], ps_tv[:, j, c * UNIT:(c + 1) * UNIT],
                                                     cur_m[:, alpha + k:alpha + k + 1], mix[n][:, k, :],
                                                     ALU.mult, ALU.add).then_inc(s_mix, 1)
                            yield
                    yield from mix_high(u, 0, j, first)

            def mix_high(u, n, j, first):
                if j == 0 and not first:
                    dve.wait_ge((s_k, s_r)[n], u * 2)
                dve.wait_ge(s_mix, u * 2 * KC + KC * j + 2 * n + 2)
                dve.tensor_copy(mixs[n][0][:, 2 * j:2 * j + 2, :], mix[n][:, 2 * j:2 * j + 2, :])\
                   .then_inc(s_mix_hi[n], 1)
                yield

            def mix_r_high(u, first):
                for j in range(2):
                    yield from mix_high(u, 1, j, first)

            def residual(b, s, first, banks=ps_cd, gated=xn2):
                u = b * UPB + s
                r = s % 4
                if s == 0:
                    dve.wait_ge(s_gate_a, b * 16 + 16)
                if not first:
                    dve.wait_ge(s_t2, u * KC)
                for i in range(TPU):
                    dve.wait_ge(s_cd, u * TPU + i + 1)
                    dve.tensor_tensor(gated[:, i, :], banks[:, i, :], gate_a[:, :], ALU.mult).then_inc(s_gated, 1)
                    yield
                dve.wait_ge(s_x2in[r], b * (UPB // 4 * 16) + s // 4 * 16 + 16)
                for i in range(TPU):
                    dve.wait_ge(s_gated, u * TPU + i + 1)
                    dve.scalar_tensor_tensor(x2[:, r, i, :], gated[:, i, :], 1.0, x2[:, r, i, :], ALU.mult, ALU.add,
                                             accum_out=sum2[:, i:i + 1]).then_inc(s_x2, 1)
                    yield

            def normalise2(b, s):
                u = b * UPB + s
                dve.wait_ge(s_rstd2, u + 1)
                for i in range(TPU):
                    dve.tensor_scalar(xn2[:, i, :], x2[:, s % 4, i, :], neg_mean2[:, i:i + 1], rstd2[:, i:i + 1],
                                      ALU.add, ALU.mult).then_inc(s_xn2, 1)
                    yield

            def k_high(u):
                for i in range(2):
                    dve.wait_ge(s_kk, u * 2 + i + 1)
                    dve.tensor_copy(kks[0][:, 2 * i:2 * i + 2, :],
                                    kk[:, i, :].rearrange("p (c t) -> p c t", c=2)).then_inc(s_kk_hi, 1)
                    yield

            def output(b, s):
                u = b * UPB + s
                if s == 0:
                    dve.wait_ge(s_gate_b, b * 16 + 16)
                for i in range(TPU):
                    dve.wait_ge(s_v, u * TPU + i + 1)
                    dve.wait_ge(s_rt, u * TPU + TPU + i + 1)
                    dve.scalar_tensor_tensor(rt[:, i, :], rt[:, i, :], 1.0, ps_tv[:, i, :], ALU.add, ALU.mult)\
                       .then_inc(s_rv, 1)
                    yield
                for i in range(TPU):
                    dve.wait_ge(s_rv, u * TPU + TPU + i + 1)
                    dve.tensor_tensor(rt[:, i, :], rt[:, i, :], gate_b[:, :], ALU.mult).then_inc(s_rvg, 1)
                    yield

            def tmp(t, *shape):
                n = int(np.prod(shape))
                if len(shape) == 3:
                    return t[:, 0:n].rearrange("p (a b c) -> p a b c", a=shape[0], b=shape[1])
                return t[:, 0:n].rearrange("p (a b) -> p a b", a=shape[0])

            def push_down(q, n, after, low, high):
                for l in range(high - 1, low - 1, -1):
                    c = HALF >> (l + 1)
                    step = 2 << l
                    frm = state[:, :, 0:HALF:step]
                    to = state[:, :, 1 << l:HALF:step]
                    if l == 0:
                        e1, h1 = ee[:, 0:HALF:2], hh[:, 0:HALF:2]
                        after(n)
                        dve.tensor_tensor(tmp0[:, 0:c], h1, frm[:, 1, :], ALU.mult).then_inc(s_rec, 1)
                        yield
                        r = tmp(tmp1, 2, c)
                        dve.tensor_tensor(r[:, 1, :], frm[:, 0, :], frm[:, 1, :], ALU.add).then_inc(s_rec, 1)
                        yield
                        after(n + 1)
                        dve.tensor_tensor(r[:, 0, :], frm[:, 0, :], tmp0[:, 0:c], ALU.subtract).then_inc(s_rec, 1)
                        yield
                        after(n + 3)
                        dve.tensor_tensor(r, r, e1.unsqueeze(1).broadcast_to([P, 2, c]), ALU.mult).then_inc(s_rec, 1)
                        yield
                        after(n + 4)
                        dve.tensor_tensor(to, r, f0[:, :, 0:HALF:2], ALU.add).then_inc(s_rec, 1)
                        yield
                        n += 5
                        continue
                    node = tree[l][:, :, :, 0:HALF >> l:2]
                    t, r = tmp(tmp0, 2, 2, c), tmp(tmp1, 2, c)
                    after(n)
                    dve.tensor_tensor(t, node[:, :, 0:2, :], frm.unsqueeze(1).broadcast_to([P, 2, 2, c]),
                                      ALU.mult).then_inc(s_rec, 1)
                    yield
                    after(n + 1)
                    dve.tensor_tensor(r, t[:, :, 0, :], t[:, :, 1, :], ALU.add).then_inc(s_rec, 1)
                    yield
                    after(n + 2)
                    dve.tensor_tensor(to, r, node[:, :, 2, :], ALU.add).then_inc(s_rec, 1)
                    yield
                    n += 3

            def recurrence_up(q, s, first_of_all):
                base = q * STEPS

                def after(n):
                    dve.wait_ge(s_rec, base + n)

                dve.wait_ge(s_pev, q + 1)
                if not first_of_all:
                    dve.wait_ge(s_xs, q)
                bias = [scan_bias[:, i:i + 1] for i in range(4)]
                dve.tensor_scalar(om_pos[:, :], om[:, :], bias[0], 0.0, ALU.add, ALU.max).then_inc(s_rec, 1)
                yield
                dve.tensor_scalar(om[:, :], om[:, :], bias[0], None, ALU.add).then_inc(s_rec, 1)
                yield
                after(2)
                dve.scalar_tensor_tensor(om_exp[:, :], om_pos[:, :], -2.0, om[:, :], ALU.mult, ALU.add)\
                   .then_inc(s_rec, 1)
                yield
                dve.tensor_scalar(f0[:, 0, :], f0[:, 0, :], bias[2], None, ALU.add).then_inc(s_rec, 1)
                yield
                dve.tensor_scalar(f0[:, 1, :], f0[:, 1, :], bias[3], 1.0 / DT, ALU.add, ALU.mult).then_inc(s_rec, 1)
                yield
                dve.wait_ge(s_zexp, q + 1)
                dve.tensor_scalar(ze[:, :], ze[:, :], EXP_CAP, 1.0, ALU.min, ALU.add).then_inc(s_rec, 1)
                yield
                yield
                dve.wait_ge(s_softln, q + 1)
                dve.tensor_tensor(om_pos[:, :], om_pos[:, :], om_exp[:, :], ALU.add).then_inc(s_rec, 1)
                yield
                after(7)
                dve.tensor_scalar(om_pos[:, :], om_pos[:, :], OMEGA_MIN, OMEGA_MAX, ALU.max, ALU.min)\
                   .then_inc(s_rec, 1)
                yield
                after(8)
                dve.scalar_tensor_tensor(hh[:, :], om_pos[:, :], DT * DT, om_pos[:, :], ALU.mult, ALU.mult)\
                   .then_inc(s_rec, 1)
                yield
                after(9)
                dve.scalar_tensor_tensor(ze[:, :], hh[:, :], 1.0, ze[:, :], ALU.add, ALU.mult).then_inc(s_rec, 1)
                yield
                after(10)
                dve.reciprocal(ee[:, :], ze[:, :]).then_inc(s_rec, 1)
                yield
                n, c = STEP_COEFFS, HALF // 2
                e1, e2, h1, h2 = (a[:, i:HALF:2] for a in (ee, hh) for i in range(2))
                f1, f2 = f0[:, :, 0:HALF:2], f0[:, :, 1:HALF:2]
                m = tree[1]
                neg_e, hf, r = tmp0[:, 0:c], tmp0[:, c:2 * c], tmp(tmp1, 2, c)
                dve.tensor_tensor(m[:, 0, 1, :], h1, h2, ALU.add).then_inc(s_rec, 1)
                yield
                dve.tensor_tensor(hf, h2, f1[:, 1, :], ALU.mult).then_inc(s_rec, 1)
                yield
                dve.tensor_tensor(r[:, 1, :], f1[:, 0, :], f1[:, 1, :], ALU.add).then_inc(s_rec, 1)
                yield
                after(n)
                dve.scalar_tensor_tensor(neg_e, e1, -1.0, e2, ALU.mult, ALU.mult).then_inc(s_rec, 1)
                yield
                after(n + 2)
                dve.tensor_tensor(r[:, 0, :], f1[:, 0, :], hf, ALU.subtract).then_inc(s_rec, 1)
                yield
                after(n + 4)
                dve.scalar_tensor_tensor(m[:, 0, 0, :], h2, -1.0, neg_e, ALU.add, ALU.mult).then_inc(s_rec, 1)
                yield
                dve.scalar_tensor_tensor(m[:, 1, 1, :], h1, -1.0, neg_e, ALU.add, ALU.mult).then_inc(s_rec, 1)
                yield
                dve.tensor_scalar(m[:, 1, 0, :], neg_e, -2.0, None, ALU.mult).then_inc(s_rec, 1)
                yield
                dve.tensor_tensor(m[:, 0, 1, :], m[:, 0, 1, :], neg_e, ALU.mult).then_inc(s_rec, 1)
                yield
                after(n + 5)
                dve.tensor_tensor(r, r, e2.unsqueeze(1).broadcast_to([P, 2, c]), ALU.mult).then_inc(s_rec, 1)
                yield
                after(n + 10)
                dve.tensor_tensor(m[:, :, 2, :], r, f2, ALU.add).then_inc(s_rec, 1)
                yield
                n += 11
                for l in range(1, LEVELS):
                    c = HALF >> (l + 1)
                    first, second = tree[l][:, :, :, 0:2 * c:2], tree[l][:, :, :, 1:2 * c:2]
                    t0, t1 = tmp(tmp0, 2, 3, c), tmp(tmp1, 2, 3, c)
                    after(n)
                    for j, t in ((0, t0), (1, t1)):
                        dve.tensor_tensor(t, second[:, :, j:j + 1, :].broadcast_to([P, 2, 3, c]),
                                          first[:, j:j + 1, :, :].broadcast_to([P, 2, 3, c]), ALU.mult)\
                           .then_inc(s_rec, 1)
                        yield
                    after(n + 2)
                    dve.tensor_tensor(tree[l + 1][:, :, :, :], t0, t1, ALU.add).then_inc(s_rec, 1)
                    yield
                    after(n + 3)
                    dve.tensor_tensor(tree[l + 1][:, :, 2, :], tree[l + 1][:, :, 2, :], second[:, :, 2, :],
                                      ALU.add).then_inc(s_rec, 1)
                    yield
                    n += 4
                root = tree[LEVELS][:, :, :, 0]
                t, r = tmp(tmp0, 2, 2), tmp1[:, 0:2]
                lo, up = slice(0, M), slice(M, 2 * M)
                after(n)
                for half, own in ((0, lo), (1, up)):
                    if half == 0 and s == 0:
                        dve.memset(state[lo, :, 0], 0.0).then_inc(s_rec, 1)
                    else:
                        other = (up, lo)[half]
                        dve.tensor_copy(state[own, :, 0], state[other, :, HALF]).then_inc(s_rec, 1)
                    n += 1
                    yield
                    after(n)
                    dve.tensor_tensor(t[own], root[own, :, 0:2], state[own, :, 0].unsqueeze(1).broadcast_to([M, 2, 2]),
                                      ALU.mult).then_inc(s_rec, 1)
                    n += 1
                    yield
                    after(n)
                    dve.tensor_tensor(r[own], t[own, :, 0], t[own, :, 1], ALU.add).then_inc(s_rec, 1)
                    n += 1
                    yield
                    after(n)
                    dve.tensor_tensor(state[own, :, HALF], r[own], root[own, :, 2], ALU.add).then_inc(s_rec, 1)
                    n += 1
                    yield
                    after(n)
                assert n == STEP_ROOTS
                yield from push_down(q, n, after, SPLIT_LEVEL, LEVELS)

            def recurrence_down(q):
                def after(n):
                    dve.wait_ge(s_rec, q * STEPS + n)

                yield from push_down(q, STEP_ROOTS + 3 * (LEVELS - SPLIT_LEVEL), after, 0, SPLIT_LEVEL)

            def recurrence(q, s, first_of_all):
                yield from recurrence_up(q, s, first_of_all)
                yield from recurrence_down(q)

            def run(*steps):
                for g in steps:
                    for _ in g:
                        pass

            def take(steps, count):
                for _ in range(count):
                    next(steps, None)

            def beside(steps, main, per):
                for _ in main:
                    take(steps, per)

            prep = [0]

            def then(ins):
                prep[0] += 1
                ins.then_inc(s_prep, 1)

            def after_prep():
                dve.wait_ge(s_prep, prep[0])

            def columns(n, out, add):
                dve.wait_ge(s_cols, n + 1)
                src = ps_tv[:, n % 2, 0:KC * B].rearrange("p (k b) -> p b k", k=KC)
                return dve.tensor_scalar(out, src, add, None, ALU.add)

            def gate(what, row, factor):
                g, sign, size = xn2[0:B, row, :], kk[0:B, 0, :], kk[0:B, 1, :]
                dve.wait_ge(s_row, MODS.index(what) + 1)
                after_prep()
                then(dve.tensor_scalar(sign, g, 0.0, 2.0, ALU.is_ge, ALU.mult))
                then(dve.scalar_tensor_tensor(size, g, -1.0, g, ALU.mult, ALU.max))
                yield
                after_prep()
                then(dve.tensor_scalar(size, size, GATE_MIN, None, ALU.max))
                then(dve.tensor_scalar(sign, sign, -1.0, factor, ALU.add, ALU.mult))
                yield
                after_prep()
                then(dve.tensor_tensor(g, sign, size, ALU.mult))
                yield
                after_prep()
                dve.sem_inc(s_gate, 1)

            def mixer_table():
                shift = tab_m[:, :, SHIFT:SHIFT + KC]
                then(dve.tensor_scalar(one_minus_mu[:, :, :], mu[:, :, :], -1.0, 1.0, ALU.mult, ALU.add))
                then(columns(2, shift, 0.0))
                then(columns(3, cb1[:, :, :], 1.0))
                yield
                after_prep()
                for at, a, col in ((A_R, cb1, mu[:, 0:1, :]), (A_K, cb1, mu[:, 1:2, :]),
                                   (B_R, cb1, one_minus_mu[:, 0:1, :]), (B_K, cb1, one_minus_mu[:, 1:2, :]),
                                   (FIRST_R, None, mu[:, 0:1, :]), (FIRST_K, None, mu[:, 1:2, :])):
                    src = shift if a is None else a[:, :, :]
                    then(dve.tensor_tensor(tab_m[:, :, at:at + KC], src, col.broadcast_to([P, B, KC]), ALU.mult))
                    yield
                after_prep()
                dve.sem_inc(s_tab_m, 1)
                new_columns(0, tab_m, cur_m, s_cur_m)
                yield

            dve.sem_inc(s_rv, TPU)
            dve.sem_inc(s_out, TPU)
            dve.wait_ge(s_silu, 1)
            then(dve.tensor_scalar(silu_c[:, :, :], silu_c[:, :, :], EXP_CAP, 1.0, ALU.min, ALU.add))
            after_prep()
            then(dve.reciprocal(silu_c[:, :, :], silu_c[:, :, :]))
            dve.wait_ge(s_const, 64)
            after_prep()
            dve.tensor_tensor(silu_c[:, :, :], silu_c[:, :, :], c_in[:, :, :], ALU.mult).then_inc(s_silu, 1)
            run(normalise(0))
            then(columns(0, tab_h[:, :, KC:2 * KC], 0.0))
            columns(1, tab_h[:, :, 0:KC], 1.0).then_inc(s_tab_h, 1)
            after_prep()
            dve.wait_ge(s_tab_h, 1)
            new_columns(0, tab_h, cur_h, s_cur_h)
            run(h_high(0, 0))
            for k in (2, 3):
                dve.wait_ge(s_h_hi, k + 1)
                dve.tensor_tensor(h[0][1][:, k, :], h_full[:, k, :], h[0][0][:, k, :].bitcast(F32), ALU.subtract)\
                   .then_inc(s_h_lo, 1)
            first, second = recurrence(0, 0, True), recurrence_up(1, 1, False)
            take(first, 12)
            beside(first, gate("ga", 0, 1.0), 3)
            beside(first, normalise(1), 2)
            beside(first, gate("gb", 1, 0.5), 3)
            take(first, 6)
            beside(first, h_high(1, 1), 2)
            run(first)
            states_high(0)
            run(normalise(2), mixer_table(), residual(0, 0, True))
            dve.wait_ge(s_mean2, 1)
            run(residual(0, 1, True, ps_kr, rt))
            beside(second, normalise2(0, 0), 1)
            dve.wait_ge(s_cut, len(CUTS))
            first = mixes(0, 0, True)
            take(first, 1)
            take(second, 8)
            run(first, mix_r_high(0, True))
            take(second, 4)
            run(h_high(2, 0))
            beside(second, normalise2(0, 1), 2)
            run(second)

            def slots(b, last):
                up = iter(())
                for s in range(UPB):
                    u, q = b * UPB + s, b * CPB + s // 2
                    next_mix = not (last and s + 1 >= UPB)
                    next_cd = not (last and s + 2 >= UPB)
                    next_unit = (b + (s + 1) // UPB, (s + 1) % UPB)
                    cd_unit = (b + (s + 2) // UPB, (s + 2) % UPB)
                    if s + 1 == UPB and not last:
                        new_columns(b + 1, tab_m, cur_m, s_cur_m)
                    mix_steps = mixes(*next_unit, False) if next_mix else iter(())
                    if s % 2 == 0:
                        down = recurrence_down(q + 1) if next_cd else iter(())
                        take(down, 10)
                        beside(down, k_high(u), 2)
                        run(down)
                        take(mix_steps, 7)
                        if next_cd:
                            states_high(q + 1)
                        run(mix_steps)
                        if not (last and s // 2 + 2 >= CPB):
                            up = recurrence_up(q + 2, (s // 2 + 2) % CPB, False)
                        take(up, EVEN_SOLO)
                        if next_mix:
                            beside(up, mix_r_high(u + 1, False), 1)
                        if next_cd:
                            beside(up, residual(*cd_unit, False), 2)
                        if not (last and s // 2 + 3 >= CPB):
                            beside(up, normalise(q + 3), 1)
                        if next_cd:
                            beside(up, normalise2(*cd_unit), 1)
                        beside(up, output(b, s), 1)
                    else:
                        if s // 2 + 3 == CPB and not last:
                            new_columns(b + 1, tab_h, cur_h, s_cur_h)
                        take(up, ODD_SOLO)
                        beside(up, k_high(u), 2)
                        beside(up, mix_steps, 1)
                        if next_cd:
                            beside(up, residual(*cd_unit, False), 2)
                        if not (last and s // 2 + 3 >= CPB):
                            beside(up, h_high(q + 3, (s // 2 + 3) % 2), 1)
                        if next_cd:
                            beside(up, normalise2(*cd_unit), 1)
                        if next_mix:
                            beside(up, mix_r_high(u + 1, False), 1)
                        beside(up, output(b, s), 2)
                        run(up)

            with dve.Fori(0, B - 1) as b:
                slots(b, False)
            slots(B - 1, True)

        @block.gpsimd
        def _(pool):
            def low(out, full, high, s_low):
                pool.tensor_tensor(out, full, high.bitcast(F32), ALU.subtract).then_inc(s_low, 1)

            def rstd_of(sq, var, rstd, index, s_sq, s_var, s_rstd):
                n = sq.shape[1]
                pool.wait_ge(s_sq, index * n + n)
                pool.tensor_tensor(var[:, :], sq[:, :], inv_d[:, 0:n], ALU.mult).then_inc(s_var, 1)
                pool.wait_ge(s_var, index * 2 + 1)
                pool.tensor_tensor(var[:, :], var[:, :], eps[:, 0:n], ALU.add).then_inc(s_var, 1)
                pool.wait_ge(s_var, index * 2 + 2)
                pool.tensor_tensor(rstd[:, :], var[:, :], minus_half[:, 0:n], ALU.pow).then_inc(s_rstd, 1)

            def rstd1_of(q):
                rstd_of(sq1, var1, rstd1, q, s_sq1, s_var1, s_rstd1)

            def rstd2_of(u):
                rstd_of(sq2, var2, rstd2, u, s_sq2, s_var2, s_rstd2)

            def h_low(q, par, ks=range(KC)):
                for k in ks:
                    pool.wait_ge(s_h_hi, q * KC + k + 1)
                    low(h[par][1][:, k, :], h_full[:, k, :], h[par][0][:, k, :], s_h_lo)

            def states_low(q):
                pool.wait_ge(s_xs_hi, q + 1)
                low(xss[1][:, :], xs[:, :], xss[0][:, :], s_xs_lo)

            def mix_low(u, n):
                for j in range(2):
                    k = slice(2 * j, 2 * j + 2)
                    pool.wait_ge(s_mix_hi[n], u * 2 + j + 1)
                    low(mixs[n][1][:, k, :], mix[n][:, k, :], mixs[n][0][:, k, :], s_mix_lo[n])

            def add_output(u, place):
                for i in range(TPU):
                    pool.wait_ge(s_rvg, u * TPU + i + 1)
                    pool.tensor_tensor(x2[:, place, i, :], x2[:, place, i, :], rt[:, i, :], ALU.add).then_inc(s_out, 1)

            def k_low(u):
                for i in range(2):
                    pool.wait_ge(s_kk_hi, u * 2 + i + 1)
                    k = slice(2 * i, 2 * i + 2)
                    low(kks[1][:, k, :], kk[:, i, :].rearrange("p (c t) -> p c t", c=2), kks[0][:, k, :], s_kk_lo)

            for c, value in ((inv_d, 1.0 / D), (eps, EPS), (minus_half, -0.5)):
                pool.memset(c[:, :], value).then_inc(s_pool_const, 1)
            pool.wait_ge(s_pool_const, 3)
            def weight_low(what):
                pool.wait_ge(s_cut_hi, CUTS.index(what) + 1)
                hi, lo, src = weight_views(what)
                pool.tensor_tensor(lo, src, hi.bitcast(F32), ALU.subtract).then_inc(s_cut, 1)

            rstd1_of(0)
            weight_low("proj")
            h_low(0, 0, (0, 1))
            weight_low("wc")
            weight_low("wd")
            rstd1_of(1)
            h_low(1, 1)
            weight_low("wr")
            weight_low("wv")
            weight_low("wk")
            rstd1_of(2)
            states_low(0)
            rstd2_of(0)
            mix_low(0, 0)
            rstd2_of(1)
            mix_low(0, 1)
            h_low(2, 0)

            def slots(b, last):
                for s in range(UPB):
                    u, q = b * UPB + s, b * CPB + s // 2
                    next_mix, next_cd = not (last and s + 1 >= UPB), not (last and s + 2 >= UPB)
                    k_low(u)
                    if next_mix:
                        mix_low(u + 1, 0)
                    if s % 2 == 0:
                        if next_cd:
                            states_low(q + 1)
                        if next_mix:
                            mix_low(u + 1, 1)
                        if not (last and s // 2 + 3 >= CPB):
                            rstd1_of(q + 3)
                        if next_cd:
                            rstd2_of(u + 2)
                    else:
                        if next_cd:
                            rstd2_of(u + 2)
                        if not (last and s // 2 + 3 >= CPB):
                            h_low(q + 3, (s // 2 + 3) % 2)
                        if next_mix:
                            mix_low(u + 1, 1)
                    add_output(u, s % 4)

            with pool.Fori(0, B - 1) as b:
                slots(b, False)
            slots(B - 1, True)


def kernel(**inputs):
    import concourse.bacc as bacc
    from concourse.bass_utils import run_bass_kernel_spmd

    def a(name):
        return np.asarray(inputs["L0_" + name])

    def t(w):
        return np.ascontiguousarray(w.T)

    b_b = a("attn_b_B")
    arrays = {
        "x": a("attn_u").reshape(B * T, D),
        "c": np.ascontiguousarray(a("c").T.reshape(KC, P, B).transpose(1, 0, 2)),
        "ident": np.eye(P, dtype=np.float32),
        "scan_bias": np.ascontiguousarray(np.stack(
            [np.tile(v, 2) for v in (a("attn_b_omega"), a("attn_b_zeta"), b_b[:M], b_b[M:])], axis=1)),
        "mu": np.ascontiguousarray(np.stack(
            [a("ffn_mu_r").reshape(KC, P).T, a("ffn_mu_k").reshape(KC, P).T], axis=1)),
        "wmod": a("wmod"),
        "w_omega": t(a("attn_W_omega")), "w_zeta": t(a("attn_W_zeta")), "w_b": t(a("attn_W_B")),
        "wd": t(a("attn_D_mat")), "wc": t(a("attn_C")),
        "wk": t(a("ffn_W_k")), "wr": t(a("ffn_W_r")), "wv": t(a("ffn_W_v")),
    }
    arrays = {k: np.ascontiguousarray(v) for k, v in arrays.items()}
    nc = bacc.Bacc("TRN2", target_bir_lowering=False, num_devices=1, dynamic_dma_scratch_size=1024)
    dram = {k: nc.dram_tensor(f"in_{k}", v.shape, F32, kind="ExternalInput").ap() for k, v in arrays.items()}
    dram["gate_rows"] = nc.dram_tensor("gate_rows", [2, B, D], F32, kind="Internal").ap()
    dram["out"] = nc.dram_tensor("out", [B * T, D], F32, kind="ExternalOutput").ap()
    build(nc, dram)
    r = run_bass_kernel_spmd(nc, [{f"in_{k}": v for k, v in arrays.items()}], core_ids=[0])
    return np.asarray(r.results[0]["out"]).reshape(B, T, D)
```

```python
from contextlib import ExitStack

import numpy as np

import concourse.bass as bass
from concourse import mybir

F32 = mybir.dt.float32
F32R = mybir.dt.float32r
ALU = mybir.AluOpType
ACT = mybir.ActivationFunctionType

B, T, D, M = 4, 2048, 512, 64
P = 128
KC = D // P
CHUNK, UNIT, HALF = 512, 256, 256
CPB = T // CHUNK
UPB = T // UNIT
NCHUNK, NUNIT = B * CPB, B * UPB
TPU, TPC = UNIT // P, CHUNK // P
TOP = 4
DT, OMEGA_MIN, OMEGA_MAX, EPS, GATE_MIN = 0.01, 1e-4, 100.0, 1e-5, 0.25
EXP_CAP = 1e30
A_R, A_K, B_R, B_K, SHIFT, FIRST_R, FIRST_K, NTAB = 0, 4, 8, 12, 16, 20, 24, 28
STEP_NEG_ABS, STEP_COEFFS = 3, 11
STEP_PREFIX = STEP_COEFFS + 11 + 4 * (TOP - 1) + 5 * ((HALF >> TOP).bit_length() - 1)
STEP_ROOTS = STEP_PREFIX + 6
STEPS = STEP_ROOTS + 2 * (TOP - 1) + 5
SPLIT_LEVEL = 3
EVEN_SOLO, ODD_SOLO, DOWN_FIRST = 8, 7, 12
EVEN_PER = {"mix_r_high": 2, "residual": 2, "normalise": 1, "normalise2": 0, "output": 1}
ODD_PER = {"k_high": 1, "mixes": 1, "residual": 1, "h_high": 2, "normalise2": 2, "mix_r_high": 2, "output": 1}
EDGES = 3 + 5 * (UPB - 1)


def build(nc, d):
    ctx = ExitStack()
    with ctx:
        def sb(name, shape, dt=F32):
            return ctx.enter_context(nc.sbuf_tensor(name, shape, dt))

        def sem(name):
            return ctx.enter_context(nc.semaphore(name))

        proj = [sb(f"proj_{n}", [P, KC, 256], F32R) for n in ("hi", "lo")]
        wd = [sb(f"wd_{n}", [P, KC, D], F32R) for n in ("hi", "lo")]
        wc = [sb(f"wc_{n}", [P, D], F32R) for n in ("hi", "lo")]
        wk = [sb(f"wk_{n}", [P, KC, D], F32R) for n in ("hi", "lo")]
        wr = [sb(f"wr_{n}", [P, KC, D], F32R) for n in ("hi", "lo")]
        wv = [sb(f"wv_{n}", [P, KC, D], F32R) for n in ("hi", "lo")]
        ident = sb("ident", [P, P])
        scan_bias = sb("scan_bias", [P, 4])
        mu = sb("mu", [P, 2, KC])
        one_minus_mu = sb("one_minus_mu", [P, 2, KC])
        silu_c = sb("silu_c", [P, KC, B])
        c_in = sb("c_in", [P, KC, B])
        tab_h = sb("tab_h", [P, B, 2 * KC])
        tab_m = sb("tab_m", [P, B, NTAB])
        cb1 = sb("cb1", [P, B, KC])
        cur_h = sb("cur_h", [P, 2 * KC])
        cur_m = sb("cur_m", [P, NTAB])
        gate_a = sb("gate_a", [P, D])
        gate_b = sb("gate_b", [P, D])
        inv_d, eps, minus_half = (sb(n, [P, TPC]) for n in ("inv_d", "eps", "minus_half"))

        x_in = sb("x_in", [P, TPC, D])
        gate_cols = sb("gate_cols", [P, 3, 2, B * D // P])
        sum1 = sb("sum1", [P, TPC])
        norm_bias1 = sb("norm_bias1", [P, TPC])
        neg_mean1 = sb("neg_mean1", [P, TPC])
        sq1 = sb("sq1", [P, TPC])
        var1 = sb("var1", [P, TPC])
        square_out = sb("square_out", [P, 2, D], mybir.dt.bfloat16)
        rstd1 = sb("rstd1", [P, TPC])
        h_full = sb("h_full", [P, KC, CHUNK])
        h = [[sb(f"h_{n}{i}", [P, KC, CHUNK], F32R) for n in ("hi", "lo")] for i in range(2)]

        x2 = sb("x2", [P, 4, TPU, D])
        sum2 = sb("sum2", [P, TPU])
        neg_mean2 = sb("neg_mean2", [P, TPU])
        sq2 = sb("sq2", [P, TPU])
        var2 = sb("var2", [P, TPU])
        rstd2 = sb("rstd2", [P, TPU])
        xn2 = sb("xn2", [P, TPU, D])
        last_n = sb("last_n", [P, KC])
        mix_full = sb("mix_full", [P, 2, KC, UNIT])
        mix = [mix_full[:, n] for n in range(2)]
        mixs = [[sb(f"mix_{n}_{w}", [P, KC, UNIT], F32R) for w in ("hi", "lo")] for n in "kr"]
        kk = sb("kk", [P, 2, 2 * UNIT])
        kks = [sb(f"kk_{m}", [P, KC, UNIT], F32R) for m in ("hi", "lo")]
        rt = sb("rt", [P, TPU, D])

        om = sb("om", [P, HALF])
        om_pos = sb("om_pos", [P, HALF])
        om_exp = sb("om_exp", [P, HALF])
        ze = sb("ze", [P, HALF])
        hh = sb("hh", [P, HALF])
        ee = sb("ee", [P, HALF])
        f0 = sb("f0", [P, 2, HALF])
        tree = [None] + [sb(f"tree{l}", [P, 2, 3, HALF >> l]) for l in range(1, TOP + 1)]
        prefix = sb("prefix", [P, 2, 2, 3, HALF >> TOP])
        tmp0 = sb("tmp0", [P, 384])
        tmp1 = sb("tmp1", [P, 384])
        state = sb("state", [P, 3, HALF + 1])
        xs = sb("xs", [P, CHUNK])
        xss = [sb(f"xs_{m}", [P, CHUNK], F32R) for m in ("hi", "lo")]

        stage = [x2[:, 0:2].rearrange("p a t n -> p (a t) n"), x2[:, 2:4].rearrange("p a t n -> p (a t) n"),
                 mix_full[:, :].rearrange("p a k t -> p (a k t)").rearrange("p (k n) -> p k n", k=KC),
                 xs[:, :].unsqueeze(1)]

        def banks(name):
            return ctx.enter_context(nc.psum_tensor(name, [P, 2, 512], F32))

        ps_kr, ps_tv, ps_pt, ps_cd = banks("ps_kr"), banks("ps_tv"), banks("ps_pt"), banks("ps_cd")

        s_c = sem("s_c")
        s_const = sem("s_const")
        s_stage = [sem(f"s_stage{i}") for i in range(len(stage))]
        s_cut_hi, s_cut = sem("s_cut_hi"), sem("s_cut")
        s_mod = sem("s_mod")
        s_row = sem("s_row")
        s_cols = sem("s_cols")
        s_tab_h, s_tab_m = sem("s_tab_h"), sem("s_tab_m")
        s_gate_in = sem("s_gate_in")
        s_gate = sem("s_gate")
        s_prep = sem("s_prep")
        s_silu = sem("s_silu")
        s_rows = sem("s_rows")
        s_gate_a, s_gate_b = sem("s_gate_a"), sem("s_gate_b")
        s_pool_const = sem("s_pool_const")
        s_cur_h, s_cur_m = sem("s_cur_h"), sem("s_cur_m")
        s_xin = sem("s_xin")
        s_sum1 = sem("s_sum1")
        s_mean1 = sem("s_mean1")
        s_sq1 = sem("s_sq1")
        s_var1 = sem("s_var1")
        s_rstd1 = sem("s_rstd1")
        s_norm_bias1 = sem("s_norm_bias1")
        s_xn1 = sem("s_xn1")
        s_t1 = sem("s_t1")
        s_h = sem("s_h")
        s_h_hi, s_h_lo = sem("s_h_hi"), sem("s_h_lo")
        s_p = sem("s_p")
        s_pev = sem("s_pev")
        s_zexp = sem("s_zexp")
        s_wexp = sem("s_wexp")
        s_softln = sem("s_softln")
        s_rec = sem("s_rec")
        s_xs = sem("s_xs")
        s_xs_hi, s_xs_lo = sem("s_xs_hi"), sem("s_xs_lo")
        s_x2in = [sem(f"s_x2in{r}") for r in range(4)]
        s_cd = sem("s_cd")
        s_gated = sem("s_gated")
        s_x2 = sem("s_x2")
        s_mean2, s_sq2, s_var2 = sem("s_mean2"), sem("s_sq2"), sem("s_var2")
        s_rstd2 = sem("s_rstd2")
        s_xn2 = sem("s_xn2")
        s_t2 = sem("s_t2")
        s_prev = sem("s_prev")
        s_edge = sem("s_edge")
        s_mix = sem("s_mix")
        s_mix_hi = [sem("s_mix_k_hi"), sem("s_mix_r_hi")]
        s_mix_lo = [sem("s_mix_k_lo"), sem("s_mix_r_lo")]
        s_k, s_r, s_v = sem("s_k"), sem("s_r"), sem("s_v")
        s_relu, s_kk = sem("s_relu"), sem("s_kk")
        s_kk_hi, s_kk_lo = sem("s_kk_hi"), sem("s_kk_lo")
        s_rt = sem("s_rt")
        s_rv = sem("s_rv")
        s_rvg = sem("s_rvg")
        s_out = sem("s_out")
        s_stored = sem("s_stored")

        x_rows = d["x"].rearrange("(q i p) n -> q p i n", p=P, i=TPC)
        x_units = d["x"].rearrange("(u i p) n -> u p i n", p=P, i=TPU)
        out_units = d["out"].rearrange("(u i p) n -> u p i n", p=P, i=TPU)
        rows = d["gate_rows"]
        rows_spread = rows.rearrange("g b (q n) -> g (b q) n", n=B * D // P)

        def mod_piece(v):
            return d["wmod"][:, v * D:(v + 1) * D].rearrange("(k p) n -> p k n", p=P)

        def weight_piece(name):
            return d[name].rearrange("(k p) n -> p k n", p=P)

        PIECES = {"sa": 0, "ca": 1, "proj": 2, "wc": 3, "wd": 0, "ga": 1, "sb": 2, "gb": 1, "wr": 0, "cb": 2,
                  "wv": 1, "wk": 2}
        MOD_PART = {"sa": 0, "ca": 1, "ga": 2, "sb": 3, "cb": 4, "gb": 5}
        MODS = [p for p in PIECES if p in MOD_PART]
        WEIGHTS = {"proj": proj, "wd": wd, "wc": wc, "wk": wk, "wr": wr, "wv": wv}
        CUTS = [p for p in PIECES if p in WEIGHTS]
        LANDED, FORMER, landed, owner = {}, {}, {}, {}
        for what, place in PIECES.items():
            landed[place] = landed.get(place, 0) + 16 * (3 if what == "proj" else 1)
            LANDED[what] = landed[place]
            FORMER[what] = owner.get(place)
            owner[place] = what

        def weight_views(what):
            hi, lo = WEIGHTS[what]
            src = stage[PIECES[what]]
            if what == "wc":
                return hi[:, :], lo[:, :], src[:, 0, :]
            return hi[:, :, :], lo[:, :, :], src[:, :, 0:hi.shape[2]]

        block = ctx.enter_context(nc.Block())

        @block.sync
        def _(sp):
            sp.dma_start(c_in[:, :, :], d["c"]).then_inc(s_c, 16)
            sp.dma_start(x_in[:, :, :], x_rows[0]).then_inc(s_xin, 16)
            for what, place in PIECES.items():
                former = FORMER[what]
                if former in MODS:
                    sp.wait_ge(s_mod, MODS.index(former) + 1)
                elif former:
                    sp.wait_ge(s_cut, CUTS.index(former) + 1)
                st, s = stage[place], s_stage[place]
                if what in MODS:
                    sp.dma_start(st, mod_piece(MOD_PART[what])).then_inc(s, 16)
                elif what == "proj":
                    for name, at, w in (("w_omega", 0, M), ("w_zeta", M, M), ("w_b", 2 * M, 2 * M)):
                        sp.dma_start(st[:, :, at:at + w], weight_piece(name)).then_inc(s, 16)
                elif what == "wc":
                    sp.dma_start(st[:, 0, :], d["wc"]).then_inc(s, 16)
                else:
                    sp.dma_start(st, weight_piece(what)).then_inc(s, 16)
                if what == "ca":
                    for small, name in ((ident[:, :], "ident"), (scan_bias[:, :], "scan_bias"), (mu[:, :, :], "mu")):
                        sp.dma_start(small, d[name]).then_inc(s_const, 16)
                if what == "wv":
                    sp.wait_ge(s_row, MODS.index("gb") + 1)
                    for g in range(2):
                        sp.dma_start(rows[g], xn2[0:B, g, :]).then_inc(s_rows, 16)
                    sp.wait_ge(s_rows, 32)
                    for g in range(2):
                        sp.dma_start(gate_cols[:, 0, g, :], rows_spread[g]).then_inc(s_gate_in, 16)
                if what in ("ga", "wk"):
                    q = 1 if what == "ga" else 2
                    sp.wait_ge(s_t1, q * KC)
                    sp.dma_start(x_in[:, :, :], x_rows[q]).then_inc(s_xin, 16)
            sp.wait_ge(s_gate, 1)
            for g in range(2):
                sp.dma_start(rows_spread[g], gate_cols[:, 0, g, :]).then_inc(s_rows, 16)
            sp.wait_ge(s_rows, 64)
            sp.dma_start(gate_a[:, :], rows[0, 0:1, :].partition_broadcast(P)).then_inc(s_gate_a, 16)
            sp.dma_start(gate_b[:, :], rows[1, 0:1, :].partition_broadcast(P)).then_inc(s_gate_b, 16)
            for u in range(3):
                sp.wait_ge(s_cut, CUTS.index("wr" if u < 2 else "wv") + 1)
                sp.dma_start(x2[:, u], x_units[u]).then_inc(s_x2in[u], 16)
            sp.wait_ge(s_t1, 3 * KC)
            sp.dma_start(x_in[:, :, :], x_rows[3]).then_inc(s_xin, 16)
            sp.sem_inc(s_stored, 16)

            def slots(b, last):
                for s in range(UPB):
                    u = b * UPB + s
                    if s == 6 and not last:
                        sp.wait_ge(s_gated, (b + 1) * (UPB * TPU))
                        sp.dma_start(gate_a[:, :], rows[0, bass.ds(b + 1, 1), :].partition_broadcast(P))\
                          .then_inc(s_gate_a, 16)
                    if not (last and s + 3 >= UPB):
                        sp.wait_ge(s_stored, u * 16 + 16)
                        sp.dma_start(x2[:, (s + 3) % 4], x_units[u + 3]).then_inc(s_x2in[(s + 3) % 4], 16)
                    if s % 2 == 1 and not (last and s // 2 + 4 >= CPB):
                        q = b * CPB + s // 2 + 4
                        sp.wait_ge(s_t1, q * KC)
                        sp.dma_start(x_in[:, :, :], x_rows[q]).then_inc(s_xin, 16)
                    sp.wait_ge(s_out, u * TPU + 2 * TPU)
                    sp.dma_start(out_units[u], x2[:, s % 4]).then_inc(s_stored, 16)
                if not last:
                    sp.dma_start(gate_b[:, :], rows[1, bass.ds(b + 1, 1), :].partition_broadcast(P))\
                      .then_inc(s_gate_b, 16)

            with sp.Fori(0, B - 1) as b:
                slots(b, False)
            slots(B - 1, True)
            sp.wait_ge(s_stored, 16 * (NUNIT + 1))

        @block.tensor
        def _(pe):
            def product(out, act, weight, acc0=True, acc1=True):
                n = len(act[0])
                mm = None
                for a, w in ((0, 0), (0, 1), (1, 0)):
                    for k in range(n):
                        mm = pe.matmul(out, act[a][k], weight[w][k],
                                       start=acc0 and a == 0 and w == 0 and k == 0,
                                       stop=acc1 and a == 1 and k == n - 1)
                return mm

            def t1_blocks(q, ks):
                for k in ks:
                    for i in range(TPC):
                        mm = pe.transpose(ps_pt[:, k % 2, i * P:(i + 1) * P],
                                          x_in[:, i, k * P:(k + 1) * P], ident[:, :])
                    mm.then_inc(s_t1, 1)

            def projections(q, par):
                pe.wait_ge(s_h_hi, q * KC + KC)
                pe.wait_ge(s_h_lo, q * KC + KC)
                for m in range(2):
                    product(ps_pt[:, m, :],
                            [[proj[w][:, k, m * P:(m + 1) * P] for k in range(KC)] for w in range(2)],
                            [[h[par][w][:, k, :] for k in range(KC)] for w in range(2)]).then_inc(s_p, 1)

            def h_part(s, banks, tiles=range(TPU)):
                par, at = (s // 2) % 2, (s % 2) * UNIT
                for i in tiles:
                    t = slice(at + i * P, at + (i + 1) * P)
                    product(banks[:, i, :], [[h[par][w][:, k, t] for k in range(KC)] for w in range(2)],
                            [[wd[w][:, k, :] for k in range(KC)] for w in range(2)], acc1=False)

            def states_part(s, banks, tiles=range(TPU)):
                for i in tiles:
                    t = slice((s % 2) * UNIT + i * P, (s % 2) * UNIT + (i + 1) * P)
                    product(banks[:, i, :], [[xss[w][:, t]] for w in range(2)],
                            [[wc[w][:, :]] for w in range(2)], acc0=False).then_inc(s_cd, 1)

            def t2_blocks(u):
                pe.wait_ge(s_xn2, u * TPU + TPU)
                for k in range(KC):
                    for i in range(TPU):
                        at = (k % 2) * UNIT + i * P
                        mm = pe.transpose(ps_tv[:, k // 2, at:at + P], xn2[:, i, k * P:(k + 1) * P],
                                          ident[:, :])
                    mm.then_inc(s_t2, 1)

            def modulation(what):
                n = MODS.index(what)
                pe.wait_ge(s_stage[PIECES[what]], LANDED[what])
                if n >= 2:
                    pe.wait_ge(s_row, n - 1)
                w = stage[PIECES[what]]
                for k in range(KC):
                    mm = pe.matmul(ps_cd[0:B, n % 2, :], silu_c[:, k, :], w[:, k, :],
                                   start=(k == 0), stop=(k == KC - 1))
                mm.then_inc(s_mod, 1)

            def row_to_columns(what, n):
                pe.wait_ge(s_row, MODS.index(what) + 1)
                if n >= 2:
                    pe.wait_ge(s_tab_h, 1)
                for k in range(KC):
                    mm = pe.transpose(ps_tv[:, n % 2, k * B:(k + 1) * B], rt[0:B, n % 2, k * P:(k + 1) * P],
                                      ident[0:B, 0:B])
                mm.then_inc(s_cols, 1)

            def rest_transposed_in(q):
                for k in (2, 3):
                    pe.wait_ge(s_h, q * KC + k - 1)
                    t1_blocks(q, (k,))

            pe.wait_ge(s_silu, 2)
            modulation("sa")
            modulation("ca")
            pe.wait_ge(s_const, 48)
            pe.wait_ge(s_xn1, TPC)
            t1_blocks(0, (0, 1))
            row_to_columns("sa", 0)
            row_to_columns("ca", 1)
            rest_transposed_in(0)
            pe.wait_ge(s_h, KC)
            pe.wait_ge(s_cut, CUTS.index("proj") + 1)
            projections(0, 0)
            modulation("ga")
            modulation("sb")
            modulation("gb")
            modulation("cb")
            row_to_columns("sb", 2)
            row_to_columns("cb", 3)
            pe.wait_ge(s_pev, 1)
            pe.wait_ge(s_xn1, 2 * TPC)
            t1_blocks(1, (0, 1))
            rest_transposed_in(1)
            pe.wait_ge(s_cut, CUTS.index("wd") + 1)
            pe.wait_ge(s_row, len(MODS))
            h_part(0, ps_cd)
            pe.wait_ge(s_h, 2 * KC)
            projections(1, 1)
            pe.wait_ge(s_xs_hi, 1)
            pe.wait_ge(s_xs_lo, 1)
            states_part(0, ps_cd)
            h_part(1, ps_kr)
            states_part(1, ps_kr)
            pe.wait_ge(s_tab_m, 1)
            t2_blocks(0)
            pe.wait_ge(s_pev, 2)
            pe.wait_ge(s_xn1, 3 * TPC)
            t1_blocks(2, (0, 1))
            rest_transposed_in(2)

            def k_product(u):
                pe.wait_ge(s_mix_hi[0], u * 2 + 2)
                pe.wait_ge(s_mix_lo[0], u * 2 + 2)
                pe.wait_ge(s_rt, u * TPU + TPU)
                for m in range(KC):
                    mm = product(ps_kr[:, m // 2, (m % 2) * UNIT:(m % 2 + 1) * UNIT],
                                 [[wk[w][:, k, m * P:(m + 1) * P] for k in range(KC)] for w in range(2)],
                                 [[mixs[0][w][:, k, :] for k in range(KC)] for w in range(2)])
                    if m % 2:
                        mm.then_inc(s_k, 1)

            def r_product(u):
                pe.wait_ge(s_mix_hi[1], u * 2 + 2)
                pe.wait_ge(s_mix_lo[1], u * 2 + 2)
                pe.wait_ge(s_relu, u * 2 + 2)
                for i in range(TPU):
                    product(ps_kr[:, i, :],
                            [[mixs[1][w][:, k, i * P:(i + 1) * P] for k in range(KC)] for w in range(2)],
                            [[wr[w][:, k, :] for k in range(KC)] for w in range(2)]).then_inc(s_r, 1)

            def v_product(u, mixes_before):
                pe.wait_ge(s_kk_hi, u * 2 + 2)
                pe.wait_ge(s_kk_lo, u * 2 + 2)
                if mixes_before:
                    pe.wait_ge(s_mix, u * 2 * KC + 4 * KC)
                else:
                    pe.wait_ge(s_rv, u * TPU + TPU)
                for i in range(TPU):
                    product(ps_tv[:, i, :],
                            [[kks[w][:, k, i * P:(i + 1) * P] for k in range(KC)] for w in range(2)],
                            [[wv[w][:, k, :] for k in range(KC)] for w in range(2)]).then_inc(s_v, 1)

            def slots(b, last):
                for s in range(UPB):
                    u, q = b * UPB + s, b * CPB + s // 2
                    t1 = s % 2 == 1 and not (last and s // 2 + 3 >= CPB)
                    if s == 0:
                        pe.wait_ge(s_cut, len(CUTS))
                        pe.wait_ge(s_gated, 2 * TPU)
                    k_product(u)
                    t2 = not (last and s + 1 >= UPB)
                    cd = not (last and s + 2 >= UPB)
                    if t2 and (s % 2 == 0 or not cd):
                        pe.wait_ge(s_rv, u * TPU + TPU)
                        t2_blocks(u + 1)
                    if s % 2 == 0:
                        if not (last and s // 2 + 2 >= CPB):
                            pe.wait_ge(s_h, q * KC + 3 * KC)
                            projections(q + 2, (s // 2) % 2)
                        r_product(u)
                    if cd:
                        pe.wait_ge(s_gated, u * TPU + 2 * TPU)
                        place = (s + 2) % UPB
                        if s % 2 == 0:
                            h_part(place, ps_cd)
                            pe.wait_ge(s_xs_hi, q + 2)
                            pe.wait_ge(s_xs_lo, q + 2)
                            states_part(place, ps_cd)
                        else:
                            h_part(place, ps_cd, (0,))
                            states_part(place, ps_cd, (0,))
                            if t1:
                                pe.wait_ge(s_xn1, q * TPC + 4 * TPC)
                                pe.wait_ge(s_pev, q + 3)
                                t1_blocks(q + 3, (0, 1))
                            pe.wait_ge(s_rv, u * TPU + TPU)
                            t2_blocks(u + 1)
                            h_part(place, ps_cd, (1,))
                            states_part(place, ps_cd, (1,))
                    if t1:
                        for k in (2, 3):
                            pe.wait_ge(s_h, q * KC + 3 * KC + k - 1)
                            t1_blocks(q + 3, (k,))
                    if s % 2 == 1:
                        r_product(u)
                    v_product(u, not (last and s + 1 >= UPB))

            with pe.Fori(0, B - 1) as b:
                slots(b, False)
            slots(B - 1, True)

        @block.scalar
        def _(act):
            def h_blocks(q, ks):
                for k in ks:
                    act.wait_ge(s_t1, q * KC + k + 1)
                    act.activation(h_full[:, k, :], ps_pt[:, k % 2, :], ACT.Identity,
                                   bias=cur_h[:, KC + k:KC + k + 1], scale=cur_h[:, k:k + 1]).then_inc(s_h, 1)

            def squares(x, neg_mean, out, count, s_sq):
                for i in range(out.shape[1]):
                    if i >= 2:
                        act.wait_ge(s_sq, count + i - 1)
                    act.activation(square_out[:, i % 2, :], x[:, i, :], ACT.Square, bias=neg_mean[:, i:i + 1],
                                   accum_out=out[:, i:i + 1]).then_inc(s_sq, 1)

            def statistics1(q):
                sums1(q)
                squares(x_in, neg_mean1, sq1, q * TPC, s_sq1)

            def sums1(q):
                act.wait_ge(s_xin, q * 16 + 16)
                for i in range(TPC):
                    act.activation(x_in[:, i, :], x_in[:, i, :], ACT.Identity, accum_out=sum1[:, i:i + 1])\
                       .then_inc(s_sum1, 1)
                act.wait_ge(s_sum1, q * TPC + TPC)
                act.activation(neg_mean1[:, :], sum1[:, :], ACT.Identity, scale=-1.0 / D).then_inc(s_mean1, 1)
                act.wait_ge(s_mean1, q + 1)

            def statistics2(b, s):
                u = b * UPB + s
                act.wait_ge(s_x2, u * TPU + TPU)
                act.activation(neg_mean2[:, :], sum2[:, :], ACT.Identity, scale=-1.0 / D).then_inc(s_mean2, 1)
                act.wait_ge(s_mean2, u + 1)
                squares(x2[:, s % 4], neg_mean2, sq2, u * TPU, s_sq2)

            def normalise1(q):
                act.wait_ge(s_norm_bias1, q)
                for i in range(TPC):
                    act.activation(x_in[:, i, :], x_in[:, i, :], ACT.Identity, bias=norm_bias1[:, i:i + 1],
                                   scale=rstd1[:, i:i + 1]).then_inc(s_xn1, 1)

            def h_high(q, par, ks=range(KC)):
                for k in ks:
                    act.wait_ge(s_h, q * KC + k + 1)
                    act.activation(h[par][0][:, k, :], h_full[:, k, :], ACT.Identity).then_inc(s_h_hi, 1)

            def projections_out(q):
                act.wait_ge(s_p, q * 2 + 2)
                for half in range(2):
                    to, cols = slice(half * M, half * M + M), slice(half * HALF, (half + 1) * HALF)
                    act.activation(om[to, :], ps_pt[0:M, 0, cols], ACT.Identity)
                    act.activation(ze[to, :], ps_pt[M:2 * M, 0, cols], ACT.Identity)
                    act.activation(f0[to, 0, :], ps_pt[0:M, 1, cols], ACT.Identity)
                    mm = act.activation(f0[to, 1, :], ps_pt[M:2 * M, 1, cols], ACT.Identity)
                mm.then_inc(s_pev, 1)

            def softplus_parts(q):
                act.wait_ge(s_pev, q + 1)
                act.activation(ze[:, :], ze[:, :], ACT.Exp, bias=scan_bias[:, 1:2]).then_inc(s_zexp, 1)
                act.wait_ge(s_rec, q * STEPS + STEP_NEG_ABS)
                act.activation(om_exp[:, :], om_exp[:, :], ACT.Exp).then_inc(s_wexp, 1)
                act.wait_ge(s_wexp, q + 1)
                act.activation(om_exp[:, :], om_exp[:, :], ACT.Ln, bias=1.0).then_inc(s_softln, 1)

            def states_out(q, first):
                act.wait_ge(s_rec, q * STEPS + STEPS)
                if not first:
                    act.wait_ge(s_xs_hi, q)
                    act.wait_ge(s_xs_lo, q)
                for half in range(2):
                    frm, cols = slice(half * M, half * M + M), slice(half * HALF, (half + 1) * HALF)
                    act.activation(xs[0:M, cols], state[frm, 0, 1:HALF + 1], ACT.Identity)
                    mm = act.activation(xs[M:2 * M, cols], state[frm, 1, 1:HALF + 1], ACT.Identity, scale=DT)
                mm.then_inc(s_xs, 1)

            def shifted(u, first):
                if not first:
                    for n in range(2):
                        act.wait_ge(s_mix_hi[n], u * 2)
                        act.wait_ge(s_mix_lo[n], u * 2)
                for j in range(2):
                    act.wait_ge(s_t2, u * KC + 2 * j + 2)
                    for n, beta in ((0, B_K), (1, B_R)):
                        for c in range(2):
                            k = 2 * j + c
                            mm = act.activation(mix[n][:, k, 1:UNIT], ps_tv[:, j, c * UNIT:(c + 1) * UNIT - 1],
                                                ACT.Identity, bias=cur_m[:, SHIFT + k:SHIFT + k + 1],
                                                scale=cur_m[:, beta + k:beta + k + 1])
                    mm.then_inc(s_prev, 1)

            def weight_high(what):
                act.wait_ge(s_stage[PIECES[what]], LANDED[what])
                hi, _, src = weight_views(what)
                act.activation(hi, src, ACT.Identity).then_inc(s_cut_hi, 1)

            def row_out(what, row):
                act.wait_ge(s_mod, MODS.index(what) + 1)
                act.activation(row, ps_cd[0:B, MODS.index(what) % 2, :], ACT.Identity).then_inc(s_row, 1)

            act.sem_inc(s_rt, TPU)
            act.wait_ge(s_c, 16)
            act.activation(silu_c[:, :, :], c_in[:, :, :], ACT.Exp, scale=-1.0).then_inc(s_silu, 1)
            statistics1(0)
            act.wait_ge(s_const, 48)
            weight_high("proj")
            row_out("sa", rt[0:B, 0, :])
            row_out("ca", rt[0:B, 1, :])
            act.wait_ge(s_cur_h, 1)
            h_blocks(0, range(KC))
            weight_high("wc")
            weight_high("wd")
            projections_out(0)
            softplus_parts(0)
            row_out("ga", xn2[0:B, 0, :])
            statistics1(1)
            act.wait_ge(s_cols, 2)
            row_out("sb", rt[0:B, 0, :])
            row_out("gb", xn2[0:B, 1, :])
            normalise1(1)
            weight_high("wr")
            row_out("cb", rt[0:B, 1, :])
            act.wait_ge(s_h_hi, KC)
            act.wait_ge(s_h_lo, KC)
            h_blocks(1, range(KC))
            h_high(1, 1)
            weight_high("wv")
            weight_high("wk")
            sums1(2)
            states_out(0, True)
            squares(x_in, neg_mean1, sq1, 2 * TPC, s_sq1)
            projections_out(1)
            softplus_parts(1)
            statistics2(0, 0)
            normalise1(2)
            act.wait_ge(s_cur_m, 1)
            act.wait_ge(s_cut, len(CUTS))
            shifted(0, True)
            act.wait_ge(s_h_hi, 2 * KC)
            act.wait_ge(s_h_lo, 2 * KC)
            h_blocks(2, (0, 1))
            act.wait_ge(s_xn2, TPU)
            statistics2(0, 1)
            act.wait_ge(s_cd, 2 * TPU)
            h_high(2, 0, (0, 1))
            h_blocks(2, (2, 3))
            h_high(2, 0, (2, 3))

            def slots(b, last):
                for s in range(UPB):
                    u = b * UPB + s
                    q = b * CPB + s // 2
                    if s % 2 == 0 and not (last and s // 2 + 3 >= CPB):
                        statistics1(q + 3)
                    act.wait_ge(s_rv, u * TPU + TPU)
                    for i in range(2):
                        act.wait_ge(s_k, u * 2 + i + 1)
                        act.activation(kk[:, i, :], ps_kr[:, i, :], ACT.Relu).then_inc(s_relu, 1)
                    for i in range(2):
                        act.wait_ge(s_relu, u * 2 + i + 1)
                        act.activation(kk[:, i, :], kk[:, i, :], ACT.Square).then_inc(s_kk, 1)
                    t1 = s % 2 == 1 and not (last and s // 2 + 3 >= CPB)
                    if t1:
                        if s // 2 + 3 == CPB:
                            act.wait_ge(s_cur_h, b + 2)
                        act.wait_ge(s_h_hi, q * KC + 3 * KC)
                        act.wait_ge(s_h_lo, q * KC + 3 * KC)
                        h_blocks(q + 3, (0, 1))
                    if s % 2 == 0 and not (last and s + 2 >= UPB):
                        states_out(q + 1, False)
                    if not (last and s + 1 >= UPB):
                        if s + 1 == UPB:
                            act.wait_ge(s_cur_m, b + 2)
                        shifted(u + 1, False)
                    p = s % 2 == 0 and not (last and s // 2 + 2 >= CPB)
                    if p:
                        projections_out(q + 2)
                    if t1:
                        h_blocks(q + 3, (2, 3))
                    act.wait_ge(s_out, u * TPU + TPU)
                    for i in range(TPU):
                        act.wait_ge(s_r, u * TPU + i + 1)
                        act.activation(rt[:, i, :], ps_kr[:, i, :], ACT.Tanh, scale=0.5).then_inc(s_rt, 1)
                    if s % 2 == 1 and not (last and s + 2 >= UPB):
                        statistics2(b + (s + 2) // UPB, (s + 2) % UPB)
                    if p:
                        softplus_parts(q + 2)
                    if s % 2 == 0 and not (last and s + 2 >= UPB):
                        statistics2(b + (s + 2) // UPB, (s + 2) % UPB)

            with act.Fori(0, B - 1) as b:
                slots(b, False)
            slots(B - 1, True)

        @block.vector
        def _(dve):
            def normalise(q):
                dve.wait_ge(s_rstd1, q + 1)
                for i in range(TPC):
                    dve.tensor_scalar(x_in[:, i, :], x_in[:, i, :], neg_mean1[:, i:i + 1], rstd1[:, i:i + 1],
                                      ALU.add, ALU.mult).then_inc(s_xn1, 1)
                    yield

            def h_high(q, par):
                if not (isinstance(q, int) and q < 2):
                    dve.wait_ge(s_cd, q * TPC - TPC)
                for k in range(KC):
                    dve.wait_ge(s_h, q * KC + k + 1)
                    dve.tensor_copy(h[par][0][:, k, :], h_full[:, k, :]).then_inc(s_h_hi, 1)
                    yield

            def states_high(q):
                dve.wait_ge(s_xs, q + 1)
                dve.tensor_copy(xss[0][:, :], xs[:, :]).then_inc(s_xs_hi, 1)

            def new_columns(b, table, cur, s_cur):
                dve.tensor_copy(cur[:, :], table[:, b, :] if isinstance(b, int)
                                else table[:, bass.ds(b, 1), :].rearrange("p a n -> p (a n)")).then_inc(s_cur, 1)

            def mixes(b, s, first):
                u = b * UPB + s
                at = b * EDGES + (0 if s == 0 else 3 + 5 * (s - 1))
                if s == 0:
                    dve.wait_ge(s_cur_m, b + 1)
                if not first:
                    for n in range(2):
                        dve.wait_ge(s_mix_lo[n], u * 2)
                cols = [mix[n][:, :, 0] for n in range(2)]
                if s == 0:
                    dve.tensor_copy(cols[0], cur_m[:, FIRST_K:FIRST_K + KC]).then_inc(s_edge, 1)
                    dve.tensor_copy(cols[1], cur_m[:, FIRST_R:FIRST_R + KC]).then_inc(s_edge, 1)
                    n_edges = 3
                else:
                    dve.tensor_tensor(cols[0], last_n[:, :], cur_m[:, B_K:B_K + KC], ALU.mult).then_inc(s_edge, 1)
                    dve.tensor_tensor(cols[1], last_n[:, :], cur_m[:, B_R:B_R + KC], ALU.mult).then_inc(s_edge, 1)
                    yield
                    for n in range(2):
                        dve.wait_ge(s_edge, at + n + 1)
                        dve.tensor_tensor(cols[n], cols[n], cur_m[:, SHIFT:SHIFT + KC], ALU.add).then_inc(s_edge, 1)
                    n_edges = 5
                yield
                dve.wait_ge(s_edge, at + n_edges - 1)
                for j in range(2):
                    dve.wait_ge(s_prev, u * 2 + j + 1)
                    if j == 1:
                        dve.tensor_copy(last_n[:, :],
                                        ps_tv[:, :, :].rearrange("p a (c t) -> p (a c) t", c=2)[:, :, UNIT - 1])\
                           .then_inc(s_edge, 1)
                        yield
                    for n, alpha in ((0, A_K), (1, A_R)):
                        for c in range(2):
                            k = 2 * j + c
                            dve.scalar_tensor_tensor(mix[n][:, k, :], ps_tv[:, j, c * UNIT:(c + 1) * UNIT],
                                                     cur_m[:, alpha + k:alpha + k + 1], mix[n][:, k, :],
                                                     ALU.mult, ALU.add).then_inc(s_mix, 1)
                            yield
                    yield from mix_high(u, 0, j, first)

            def mix_high(u, n, j, first):
                if j == 0 and not first:
                    dve.wait_ge((s_k, s_r)[n], u * 2)
                dve.wait_ge(s_mix, u * 2 * KC + KC * j + 2 * n + 2)
                dve.tensor_copy(mixs[n][0][:, 2 * j:2 * j + 2, :], mix[n][:, 2 * j:2 * j + 2, :])\
                   .then_inc(s_mix_hi[n], 1)
                yield

            def mix_r_high(u, first):
                for j in range(2):
                    yield from mix_high(u, 1, j, first)

            def residual(b, s, first, banks=ps_cd, gated=xn2):
                u = b * UPB + s
                r = s % 4
                if s == 0:
                    dve.wait_ge(s_gate_a, b * 16 + 16)
                if not first:
                    dve.wait_ge(s_t2, u * KC)
                for i in range(TPU):
                    dve.wait_ge(s_cd, u * TPU + i + 1)
                    dve.tensor_tensor(gated[:, i, :], banks[:, i, :], gate_a[:, :], ALU.mult).then_inc(s_gated, 1)
                    yield
                dve.wait_ge(s_x2in[r], b * (UPB // 4 * 16) + s // 4 * 16 + 16)
                for i in range(TPU):
                    dve.wait_ge(s_gated, u * TPU + i + 1)
                    dve.scalar_tensor_tensor(x2[:, r, i, :], gated[:, i, :], 1.0, x2[:, r, i, :], ALU.mult, ALU.add,
                                             accum_out=sum2[:, i:i + 1]).then_inc(s_x2, 1)
                    yield

            def normalise2(b, s):
                u = b * UPB + s
                dve.wait_ge(s_rstd2, u + 1)
                for i in range(TPU):
                    dve.tensor_scalar(xn2[:, i, :], x2[:, s % 4, i, :], neg_mean2[:, i:i + 1], rstd2[:, i:i + 1],
                                      ALU.add, ALU.mult).then_inc(s_xn2, 1)
                    yield

            def k_high(u):
                for i in range(2):
                    dve.wait_ge(s_kk, u * 2 + i + 1)
                    dve.tensor_copy(kks[0][:, 2 * i:2 * i + 2, :],
                                    kk[:, i, :].rearrange("p (c t) -> p c t", c=2)).then_inc(s_kk_hi, 1)
                    yield

            def output(b, s):
                u = b * UPB + s
                if s == 0:
                    dve.wait_ge(s_gate_b, b * 16 + 16)
                for i in range(TPU):
                    dve.wait_ge(s_v, u * TPU + i + 1)
                    dve.wait_ge(s_rt, u * TPU + TPU + i + 1)
                    dve.scalar_tensor_tensor(rt[:, i, :], rt[:, i, :], 1.0, ps_tv[:, i, :], ALU.add, ALU.mult)\
                       .then_inc(s_rv, 1)
                    yield
                for i in range(TPU):
                    dve.wait_ge(s_rv, u * TPU + TPU + i + 1)
                    dve.tensor_tensor(rt[:, i, :], rt[:, i, :], gate_b[:, :], ALU.mult).then_inc(s_rvg, 1)
                    yield

            def tmp(t, *shape):
                n = int(np.prod(shape))
                if len(shape) == 3:
                    return t[:, 0:n].rearrange("p (a b c) -> p a b c", a=shape[0], b=shape[1])
                return t[:, 0:n].rearrange("p (a b) -> p a b", a=shape[0])

            def push_down(q, n, after, low, high):
                for l in range(high - 1, low - 1, -1):
                    c = HALF >> (l + 1)
                    step = 2 << l
                    frm = state[:, :, 0:HALF:step]
                    to = state[:, :, 1 << l:HALF:step]
                    if l == 0:
                        e1, h1 = ee[:, 0:HALF:2], hh[:, 0:HALF:2]
                        after(n)
                        dve.tensor_tensor(tmp0[:, 0:c], h1, frm[:, 1, :], ALU.mult).then_inc(s_rec, 1)
                        yield
                        r = tmp(tmp1, 2, c)
                        dve.tensor_tensor(r[:, 1, :], frm[:, 0, :], frm[:, 1, :], ALU.add).then_inc(s_rec, 1)
                        yield
                        after(n + 1)
                        dve.tensor_tensor(r[:, 0, :], frm[:, 0, :], tmp0[:, 0:c], ALU.subtract).then_inc(s_rec, 1)
                        yield
                        after(n + 3)
                        dve.tensor_tensor(r, r, e1.unsqueeze(1).broadcast_to([P, 2, c]), ALU.mult).then_inc(s_rec, 1)
                        yield
                        after(n + 4)
                        dve.tensor_tensor(to[:, 0:2], r, f0[:, :, 0:HALF:2], ALU.add).then_inc(s_rec, 1)
                        yield
                        n += 5
                        continue
                    node = tree[l][:, :, :, 0:HALF >> l:2]
                    t = tmp(tmp0, 2, 3, c)
                    after(n)
                    dve.tensor_tensor(t, node, frm.unsqueeze(1).broadcast_to([P, 2, 3, c]), ALU.mult)\
                       .then_inc(s_rec, 1)
                    yield
                    after(n + 1)
                    dve.tensor_reduce(to[:, 0:2], t.rearrange("p i j c -> p i c j"), mybir.AxisListType.X, ALU.add)\
                       .then_inc(s_rec, 1)
                    yield
                    n += 2

            def recurrence_up(q, s, first_of_all):
                base = q * STEPS

                def after(n):
                    dve.wait_ge(s_rec, base + n)

                dve.wait_ge(s_pev, q + 1)
                if not first_of_all:
                    dve.wait_ge(s_xs, q)
                bias = [scan_bias[:, i:i + 1] for i in range(4)]
                dve.tensor_scalar(om_pos[:, :], om[:, :], bias[0], 0.0, ALU.add, ALU.max).then_inc(s_rec, 1)
                yield
                dve.tensor_scalar(om[:, :], om[:, :], bias[0], None, ALU.add).then_inc(s_rec, 1)
                yield
                after(2)
                dve.scalar_tensor_tensor(om_exp[:, :], om_pos[:, :], -2.0, om[:, :], ALU.mult, ALU.add)\
                   .then_inc(s_rec, 1)
                yield
                dve.tensor_scalar(f0[:, 0, :], f0[:, 0, :], bias[2], None, ALU.add).then_inc(s_rec, 1)
                yield
                dve.tensor_scalar(f0[:, 1, :], f0[:, 1, :], bias[3], 1.0 / DT, ALU.add, ALU.mult).then_inc(s_rec, 1)
                yield
                dve.wait_ge(s_zexp, q + 1)
                dve.tensor_scalar(ze[:, :], ze[:, :], EXP_CAP, 1.0, ALU.min, ALU.add).then_inc(s_rec, 1)
                yield
                yield
                dve.wait_ge(s_softln, q + 1)
                dve.tensor_tensor(om_pos[:, :], om_pos[:, :], om_exp[:, :], ALU.add).then_inc(s_rec, 1)
                yield
                after(7)
                dve.tensor_scalar(om_pos[:, :], om_pos[:, :], OMEGA_MIN, OMEGA_MAX, ALU.max, ALU.min)\
                   .then_inc(s_rec, 1)
                yield
                after(8)
                dve.scalar_tensor_tensor(hh[:, :], om_pos[:, :], DT * DT, om_pos[:, :], ALU.mult, ALU.mult)\
                   .then_inc(s_rec, 1)
                yield
                after(9)
                dve.scalar_tensor_tensor(ze[:, :], hh[:, :], 1.0, ze[:, :], ALU.add, ALU.mult).then_inc(s_rec, 1)
                yield
                after(10)
                dve.reciprocal(ee[:, :], ze[:, :]).then_inc(s_rec, 1)
                yield
                n, c = STEP_COEFFS, HALF // 2
                e1, e2, h1, h2 = (a[:, i:HALF:2] for a in (ee, hh) for i in range(2))
                f1, f2 = f0[:, :, 0:HALF:2], f0[:, :, 1:HALF:2]
                m = tree[1]
                neg_e, hf, r = tmp0[:, 0:c], tmp0[:, c:2 * c], tmp(tmp1, 2, c)
                dve.tensor_tensor(m[:, 0, 1, :], h1, h2, ALU.add).then_inc(s_rec, 1)
                yield
                dve.tensor_tensor(hf, h2, f1[:, 1, :], ALU.mult).then_inc(s_rec, 1)
                yield
                dve.tensor_tensor(r[:, 1, :], f1[:, 0, :], f1[:, 1, :], ALU.add).then_inc(s_rec, 1)
                yield
                after(n)
                dve.scalar_tensor_tensor(neg_e, e1, -1.0, e2, ALU.mult, ALU.mult).then_inc(s_rec, 1)
                yield
                after(n + 2)
                dve.tensor_tensor(r[:, 0, :], f1[:, 0, :], hf, ALU.subtract).then_inc(s_rec, 1)
                yield
                after(n + 4)
                dve.scalar_tensor_tensor(m[:, 0, 0, :], h2, -1.0, neg_e, ALU.add, ALU.mult).then_inc(s_rec, 1)
                yield
                dve.scalar_tensor_tensor(m[:, 1, 1, :], h1, -1.0, neg_e, ALU.add, ALU.mult).then_inc(s_rec, 1)
                yield
                dve.tensor_scalar(m[:, 1, 0, :], neg_e, -2.0, None, ALU.mult).then_inc(s_rec, 1)
                yield
                dve.tensor_tensor(m[:, 0, 1, :], m[:, 0, 1, :], neg_e, ALU.mult).then_inc(s_rec, 1)
                yield
                after(n + 5)
                dve.tensor_tensor(r, r, e2.unsqueeze(1).broadcast_to([P, 2, c]), ALU.mult).then_inc(s_rec, 1)
                yield
                after(n + 10)
                dve.tensor_tensor(m[:, :, 2, :], r, f2, ALU.add).then_inc(s_rec, 1)
                yield
                n += 11
                for l in range(1, TOP):
                    c = HALF >> (l + 1)
                    first, second = tree[l][:, :, :, 0:2 * c:2], tree[l][:, :, :, 1:2 * c:2]
                    t0, t1 = tmp(tmp0, 2, 3, c), tmp(tmp1, 2, 3, c)
                    after(n)
                    for j, t in ((0, t0), (1, t1)):
                        dve.tensor_tensor(t, second[:, :, j:j + 1, :].broadcast_to([P, 2, 3, c]),
                                          first[:, j:j + 1, :, :].broadcast_to([P, 2, 3, c]), ALU.mult)\
                           .then_inc(s_rec, 1)
                        yield
                    after(n + 2)
                    dve.tensor_tensor(tree[l + 1][:, :, :, :], t0, t1, ALU.add).then_inc(s_rec, 1)
                    yield
                    after(n + 3)
                    dve.tensor_tensor(tree[l + 1][:, :, 2, :], tree[l + 1][:, :, 2, :], second[:, :, 2, :],
                                      ALU.add).then_inc(s_rec, 1)
                    yield
                    n += 4
                cur, c, reach, turn = tree[TOP][:, :, :, :], HALF >> TOP, 1, 0
                while reach < c:
                    new, w = prefix[:, turn % 2], c - reach
                    first, second = cur[:, :, :, 0:w], cur[:, :, :, reach:c]
                    t0, t1 = tmp(tmp0, 2, 3, w), tmp(tmp1, 2, 3, w)
                    after(n)
                    for j, t in ((0, t0), (1, t1)):
                        dve.tensor_tensor(t, second[:, :, j:j + 1, :].broadcast_to([P, 2, 3, w]),
                                          first[:, j:j + 1, :, :].broadcast_to([P, 2, 3, w]), ALU.mult)\
                           .then_inc(s_rec, 1)
                        yield
                    dve.tensor_copy(new[:, :, :, 0:reach], cur[:, :, :, 0:reach]).then_inc(s_rec, 1)
                    yield
                    after(n + 2)
                    dve.tensor_tensor(new[:, :, :, reach:c], t0, t1, ALU.add).then_inc(s_rec, 1)
                    yield
                    after(n + 4)
                    dve.tensor_tensor(new[:, :, 2, reach:c], new[:, :, 2, reach:c], second[:, :, 2, :], ALU.add)\
                       .then_inc(s_rec, 1)
                    yield
                    cur, reach, turn, n = new, 2 * reach, turn + 1, n + 5
                assert n == STEP_PREFIX
                t = tmp(tmp0, 2, 3)
                lo, up = slice(0, M), slice(M, 2 * M)
                after(n)
                if s == 0:
                    dve.memset(state[lo, 0:2, 0], 0.0).then_inc(s_rec, 1)
                else:
                    dve.tensor_copy(state[lo, 0:2, 0], state[up, 0:2, HALF]).then_inc(s_rec, 1)
                yield
                after(n + 1)
                dve.tensor_tensor(t[lo], cur[lo, :, :, c - 1], state[lo, :, 0].unsqueeze(1).broadcast_to([M, 2, 3]),
                                  ALU.mult).then_inc(s_rec, 1)
                yield
                after(n + 2)
                dve.tensor_reduce(state[lo, 0:2, HALF], t[lo], mybir.AxisListType.X, ALU.add).then_inc(s_rec, 1)
                yield
                after(n + 3)
                dve.tensor_copy(state[up, 0:2, 0], state[lo, 0:2, HALF]).then_inc(s_rec, 1)
                yield
                t = tmp(tmp1, 2, 3, c)
                after(n + 4)
                dve.tensor_tensor(t, cur, state[:, :, 0:1].unsqueeze(1).broadcast_to([P, 2, 3, c]), ALU.mult)\
                   .then_inc(s_rec, 1)
                yield
                after(n + 5)
                dve.tensor_reduce(state[:, 0:2, HALF // c:HALF + 1:HALF // c], t.rearrange("p i j c -> p i c j"),
                                  mybir.AxisListType.X, ALU.add).then_inc(s_rec, 1)
                yield
                n += 6
                after(n)
                assert n == STEP_ROOTS
                yield from push_down(q, n, after, SPLIT_LEVEL, TOP)

            def recurrence_down(q):
                def after(n):
                    dve.wait_ge(s_rec, q * STEPS + n)

                yield from push_down(q, STEP_ROOTS + 2 * (TOP - SPLIT_LEVEL), after, 0, SPLIT_LEVEL)

            def recurrence(q, s, first_of_all):
                yield from recurrence_up(q, s, first_of_all)
                yield from recurrence_down(q)

            def run(*steps):
                for g in steps:
                    for _ in g:
                        pass

            def take(steps, count):
                for _ in range(count):
                    next(steps, None)

            def beside(steps, main, per):
                for _ in main:
                    take(steps, per)

            prep = [0]

            def then(ins):
                prep[0] += 1
                ins.then_inc(s_prep, 1)

            def after_prep():
                dve.wait_ge(s_prep, prep[0])

            def columns(n, out, add):
                dve.wait_ge(s_cols, n + 1)
                src = ps_tv[:, n % 2, 0:KC * B].rearrange("p (k b) -> p b k", k=KC)
                return dve.tensor_scalar(out, src, add, None, ALU.add)

            def gates():
                g, sign, size = gate_cols[:, 0], gate_cols[:, 1], gate_cols[:, 2]
                dve.wait_ge(s_gate_in, 32)
                after_prep()
                then(dve.tensor_scalar(sign, g, 0.0, 2.0, ALU.is_ge, ALU.mult))
                then(dve.scalar_tensor_tensor(size, g, -1.0, g, ALU.mult, ALU.max))
                yield
                after_prep()
                then(dve.tensor_scalar(size, size, GATE_MIN, None, ALU.max))
                then(dve.tensor_scalar(sign[:, 0], sign[:, 0], -1.0, 1.0, ALU.add, ALU.mult))
                then(dve.tensor_scalar(sign[:, 1], sign[:, 1], -1.0, 0.5, ALU.add, ALU.mult))
                yield
                after_prep()
                dve.tensor_tensor(g, sign, size, ALU.mult).then_inc(s_gate, 1)
                yield

            def mixer_table():
                shift = tab_m[:, :, SHIFT:SHIFT + KC]
                then(dve.tensor_scalar(one_minus_mu[:, :, :], mu[:, :, :], -1.0, 1.0, ALU.mult, ALU.add))
                then(columns(2, shift, 0.0))
                then(columns(3, cb1[:, :, :], 1.0))
                yield
                after_prep()
                for at, a, col in ((A_R, cb1, mu[:, 0:1, :]), (A_K, cb1, mu[:, 1:2, :]),
                                   (B_R, cb1, one_minus_mu[:, 0:1, :]), (B_K, cb1, one_minus_mu[:, 1:2, :]),
                                   (FIRST_R, None, mu[:, 0:1, :]), (FIRST_K, None, mu[:, 1:2, :])):
                    src = shift if a is None else a[:, :, :]
                    then(dve.tensor_tensor(tab_m[:, :, at:at + KC], src, col.broadcast_to([P, B, KC]), ALU.mult))
                    yield
                after_prep()
                dve.sem_inc(s_tab_m, 1)
                new_columns(0, tab_m, cur_m, s_cur_m)
                yield

            then(dve.memset(state[:, 2, :], 1.0))
            dve.sem_inc(s_rv, TPU)
            dve.sem_inc(s_out, TPU)
            dve.wait_ge(s_silu, 1)
            then(dve.tensor_scalar(silu_c[:, :, :], silu_c[:, :, :], EXP_CAP, 1.0, ALU.min, ALU.add))
            after_prep()
            then(dve.reciprocal(silu_c[:, :, :], silu_c[:, :, :]))
            after_prep()
            dve.tensor_tensor(silu_c[:, :, :], silu_c[:, :, :], c_in[:, :, :], ALU.mult).then_inc(s_silu, 1)
            dve.wait_ge(s_const, 48)
            run(normalise(0))
            then(columns(0, tab_h[:, :, KC:2 * KC], 0.0))
            columns(1, tab_h[:, :, 0:KC], 1.0).then_inc(s_tab_h, 1)
            after_prep()
            dve.wait_ge(s_tab_h, 1)
            new_columns(0, tab_h, cur_h, s_cur_h)
            run(h_high(0, 0))
            for k in (2, 3):
                dve.wait_ge(s_h_hi, k + 1)
                dve.tensor_tensor(h[0][1][:, k, :], h_full[:, k, :], h[0][0][:, k, :].bitcast(F32), ALU.subtract)\
                   .then_inc(s_h_lo, 1)
            first, second = recurrence(0, 0, True), recurrence_up(1, 1, False)
            take(first, 40)
            beside(first, gates(), 3)
            run(first)
            states_high(0)
            run(mixer_table(), residual(0, 0, True))
            take(second, 12)
            run(normalise2(0, 0))
            run(residual(0, 1, True, ps_kr, rt))
            dve.wait_ge(s_cut, len(CUTS))
            first_mixes = mixes(0, 0, True)
            take(first_mixes, 1)
            take(second, 6)
            run(first_mixes, mix_r_high(0, True))
            take(second, 6)
            beside(second, normalise2(0, 1), 2)
            run(second)

            def slots(b, last):
                up = iter(())
                for s in range(UPB):
                    u, q = b * UPB + s, b * CPB + s // 2
                    next_mix = not (last and s + 1 >= UPB)
                    next_cd = not (last and s + 2 >= UPB)
                    next_unit = (b + (s + 1) // UPB, (s + 1) % UPB)
                    cd_unit = (b + (s + 2) // UPB, (s + 2) % UPB)
                    if s + 1 == UPB and not last:
                        new_columns(b + 1, tab_m, cur_m, s_cur_m)
                    mix_steps = mixes(*next_unit, False) if next_mix else iter(())
                    if s % 2 == 0:
                        down = recurrence_down(q + 1) if next_cd else iter(())
                        take(down, DOWN_FIRST)
                        beside(down, k_high(u), 2)
                        run(down)
                        if next_cd:
                            states_high(q + 1)
                        run(mix_steps)
                        if not (last and s // 2 + 2 >= CPB):
                            up = recurrence_up(q + 2, (s // 2 + 2) % CPB, False)
                        take(up, EVEN_SOLO)
                        if next_mix:
                            beside(up, mix_r_high(u + 1, False), EVEN_PER["mix_r_high"])
                        if next_cd:
                            beside(up, residual(*cd_unit, False), EVEN_PER["residual"])
                        if not (last and s // 2 + 3 >= CPB):
                            beside(up, normalise(q + 3), EVEN_PER["normalise"])
                        if next_cd:
                            beside(up, normalise2(*cd_unit), EVEN_PER["normalise2"])
                        beside(up, output(b, s), EVEN_PER["output"])
                    else:
                        if s // 2 + 3 == CPB and not last:
                            new_columns(b + 1, tab_h, cur_h, s_cur_h)
                        take(up, ODD_SOLO)
                        beside(up, k_high(u), ODD_PER["k_high"])
                        beside(up, mix_steps, ODD_PER["mixes"])
                        if next_cd:
                            beside(up, residual(*cd_unit, False), ODD_PER["residual"])
                        if not (last and s // 2 + 3 >= CPB):
                            beside(up, h_high(q + 3, (s // 2 + 3) % 2), ODD_PER["h_high"])
                        if next_cd:
                            beside(up, normalise2(*cd_unit), ODD_PER["normalise2"])
                        if next_mix:
                            beside(up, mix_r_high(u + 1, False), ODD_PER["mix_r_high"])
                        beside(up, output(b, s), ODD_PER["output"])
                        run(up)

            with dve.Fori(0, B - 1) as b:
                slots(b, False)
            slots(B - 1, True)

        @block.gpsimd
        def _(pool):
            def low(out, full, high, s_low):
                pool.tensor_tensor(out, full, high.bitcast(F32), ALU.subtract).then_inc(s_low, 1)

            def rstd_of(sq, var, rstd, index, s_sq, s_var, s_rstd):
                n = sq.shape[1]
                pool.wait_ge(s_sq, index * n + n)
                pool.tensor_tensor(var[:, :], sq[:, :], inv_d[:, 0:n], ALU.mult).then_inc(s_var, 1)
                pool.wait_ge(s_var, index * 2 + 1)
                pool.tensor_tensor(var[:, :], var[:, :], eps[:, 0:n], ALU.add).then_inc(s_var, 1)
                pool.wait_ge(s_var, index * 2 + 2)
                pool.tensor_tensor(rstd[:, :], var[:, :], minus_half[:, 0:n], ALU.pow).then_inc(s_rstd, 1)

            def rstd1_of(q):
                rstd_of(sq1, var1, rstd1, q, s_sq1, s_var1, s_rstd1)

            def rstd2_of(u):
                rstd_of(sq2, var2, rstd2, u, s_sq2, s_var2, s_rstd2)

            def h_low(q, par, ks=range(KC)):
                for k in ks:
                    pool.wait_ge(s_h_hi, q * KC + k + 1)
                    low(h[par][1][:, k, :], h_full[:, k, :], h[par][0][:, k, :], s_h_lo)

            def states_low(q):
                pool.wait_ge(s_xs_hi, q + 1)
                low(xss[1][:, :], xs[:, :], xss[0][:, :], s_xs_lo)

            def mix_low(u, n):
                for j in range(2):
                    k = slice(2 * j, 2 * j + 2)
                    pool.wait_ge(s_mix_hi[n], u * 2 + j + 1)
                    low(mixs[n][1][:, k, :], mix[n][:, k, :], mixs[n][0][:, k, :], s_mix_lo[n])

            def add_output(u, place):
                for i in range(TPU):
                    pool.wait_ge(s_rvg, u * TPU + i + 1)
                    pool.tensor_tensor(x2[:, place, i, :], x2[:, place, i, :], rt[:, i, :], ALU.add).then_inc(s_out, 1)

            def k_low(u):
                for i in range(2):
                    pool.wait_ge(s_kk_hi, u * 2 + i + 1)
                    k = slice(2 * i, 2 * i + 2)
                    low(kks[1][:, k, :], kk[:, i, :].rearrange("p (c t) -> p c t", c=2), kks[0][:, k, :], s_kk_lo)

            for c, value in ((inv_d, 1.0 / D), (eps, EPS), (minus_half, -0.5)):
                pool.memset(c[:, :], value).then_inc(s_pool_const, 1)
            pool.wait_ge(s_pool_const, 3)
            def norm_bias(q):
                pool.wait_ge(s_rstd1, q + 1)
                pool.tensor_tensor(norm_bias1[:, :], neg_mean1[:, :], rstd1[:, :], ALU.mult).then_inc(s_norm_bias1, 1)

            def weight_low(what):
                pool.wait_ge(s_cut_hi, CUTS.index(what) + 1)
                hi, lo, src = weight_views(what)
                pool.tensor_tensor(lo, src, hi.bitcast(F32), ALU.subtract).then_inc(s_cut, 1)

            rstd1_of(0)
            weight_low("proj")
            h_low(0, 0, (0, 1))
            weight_low("wc")
            weight_low("wd")
            rstd1_of(1)
            norm_bias(1)
            weight_low("wr")
            h_low(1, 1)
            weight_low("wv")
            states_low(0)
            weight_low("wk")
            rstd1_of(2)
            norm_bias(2)
            rstd2_of(0)
            mix_low(0, 0)
            rstd2_of(1)
            mix_low(0, 1)
            h_low(2, 0)

            def slots(b, last):
                for s in range(UPB):
                    u, q = b * UPB + s, b * CPB + s // 2
                    next_mix, next_cd = not (last and s + 1 >= UPB), not (last and s + 2 >= UPB)
                    if s % 2 == 0 and not (last and s // 2 + 3 >= CPB):
                        rstd1_of(q + 3)
                    k_low(u)
                    if s % 2 == 0 and next_cd:
                        states_low(q + 1)
                    if next_mix:
                        mix_low(u + 1, 0)
                    if s % 2 == 0:
                        if next_mix:
                            mix_low(u + 1, 1)
                        if next_cd:
                            rstd2_of(u + 2)
                    else:
                        t1 = not (last and s // 2 + 3 >= CPB)
                        if t1:
                            h_low(q + 3, (s // 2 + 3) % 2, (0,))
                        if next_cd:
                            rstd2_of(u + 2)
                        if t1:
                            h_low(q + 3, (s // 2 + 3) % 2, (1, 2, 3))
                        if next_mix:
                            mix_low(u + 1, 1)
                    add_output(u, s % 4)

            with pool.Fori(0, B - 1) as b:
                slots(b, False)
            slots(B - 1, True)


def kernel(**inputs):
    import concourse.bacc as bacc
    from concourse.bass_utils import run_bass_kernel_spmd

    def a(name):
        return np.asarray(inputs["L0_" + name])

    def t(w):
        return np.ascontiguousarray(w.T)

    b_b = a("attn_b_B")
    arrays = {
        "x": a("attn_u").reshape(B * T, D),
        "c": np.ascontiguousarray(a("c").T.reshape(KC, P, B).transpose(1, 0, 2)),
        "ident": np.eye(P, dtype=np.float32),
        "scan_bias": np.ascontiguousarray(np.stack(
            [np.tile(v, 2) for v in (a("attn_b_omega"), a("attn_b_zeta"), b_b[:M], b_b[M:])], axis=1)),
        "mu": np.ascontiguousarray(np.stack(
            [a("ffn_mu_r").reshape(KC, P).T, a("ffn_mu_k").reshape(KC, P).T], axis=1)),
        "wmod": a("wmod"),
        "w_omega": t(a("attn_W_omega")), "w_zeta": t(a("attn_W_zeta")), "w_b": t(a("attn_W_B")),
        "wd": t(a("attn_D_mat")), "wc": t(a("attn_C")),
        "wk": t(a("ffn_W_k")), "wr": t(a("ffn_W_r")), "wv": t(a("ffn_W_v")),
    }
    arrays = {k: np.ascontiguousarray(v) for k, v in arrays.items()}
    nc = bacc.Bacc("TRN2", target_bir_lowering=False, num_devices=1, dynamic_dma_scratch_size=1024)
    dram = {k: nc.dram_tensor(f"in_{k}", v.shape, F32, kind="ExternalInput").ap() for k, v in arrays.items()}
    dram["gate_rows"] = nc.dram_tensor("gate_rows", [2, B, D], F32, kind="Internal").ap()
    dram["out"] = nc.dram_tensor("out", [B * T, D], F32, kind="ExternalOutput").ap()
    build(nc, dram)
    r = run_bass_kernel_spmd(nc, [{f"in_{k}": v for k, v in arrays.items()}], core_ids=[0])
    return np.asarray(r.results[0]["out"]).reshape(B, T, D)
```
